# Optimizing a Trainium2 kernel written in Bass

```python
import numpy as np
import jax
import jax.numpy as jnp

def _softmax(x, axis=-1):
    return jax.nn.softmax(x, axis=axis)

def _gelu(x):
    return jax.nn.gelu(x, approximate=True)

def _silu(x):
    return jax.nn.silu(x)

def _sigmoid(x):
    return jax.nn.sigmoid(x)

def _layernorm(x, axis=-1, eps=1e-05):
    m = jnp.mean(x, axis=axis, keepdims=True)
    v = jnp.var(x, axis=axis, keepdims=True)
    return (x - m) / jnp.sqrt(v + eps)

def _scatter_add(tgt, idx, src, axis=0):
    return tgt.at[idx].add(src)

def _segment_sum(src, seg, n):
    return jax.ops.segment_sum(src, seg, n)
kernel_name = 'mk_vit_tower_cls_d2_tok_img768_r4_21bc3a'

def setup_inputs(seed: int=0):
    np.random.seed(seed)
    _w = jnp.asarray

    def _rec_inputs():
        import jax
        import jax.numpy as jnp
        _rk = jax.random.key(seed)
        x = 7.57192e-06 + 1.00007 * jax.random.normal(jax.random.fold_in(_rk, 1), (8, 224, 224, 3), jnp.float32)
        cls_tok = 0.02 * jax.random.normal(jax.random.fold_in(_rk, 5), (1, 1, 192), jnp.float32)
        return (x, cls_tok)
    x, cls_tok = _rec_inputs()

    def _L0_tok_setup():
        import jax, jax.numpy as jnp
        import numpy as np
        PATCH_SIZES = (8, 16, 32)
        PROJ_DIM = 192
        C = 3

        def _extract_patches(images, p):
            B, H, W, Cc = images.shape
            nh, nw = (H // p, W // p)
            x = images.reshape(B, nh, p, nw, p, Cc)
            x = x.transpose(0, 1, 3, 2, 4, 5)
            return x.reshape(B, nh * nw, p * p * Cc)
        key = jax.random.key(seed)
        ks = jax.random.split(key, 1 + 2 * len(PATCH_SIZES))
        images = jax.random.normal(ks[0], (64, 224, 224, C), dtype=jnp.float32)
        inp = {'images': images}
        for i, p in enumerate(PATCH_SIZES):
            k_in = p * p * C
            scale = 1.0 / np.sqrt(k_in)
            inp[f'W{i}'] = jax.random.uniform(ks[1 + 2 * i], (k_in, PROJ_DIM), dtype=jnp.float32, minval=-scale, maxval=scale)
            inp[f'b{i}'] = jnp.zeros((PROJ_DIM,), dtype=jnp.float32)
        return inp
    _L0_tok_all = _L0_tok_setup()
    _L0_tok_in = {k: v for k, v in _L0_tok_all.items() if k in ('W0', 'b0', 'W1', 'b1', 'W2', 'b2')}
    del _L0_tok_all

    def _L0_attn_setup():
        import jax, jax.numpy as jnp
        import numpy as np
        EMBED_DIM = 192
        MAX_LEN = 256
        ALPHA = 0.99
        BATCH = 16

        def _retention_mask(sl, alpha, dtype):
            i = jnp.arange(sl)[:, None]
            j = jnp.arange(sl)[None, :]
            causal = i >= j
            exponent = jnp.where(causal, (i - j).astype(dtype), 0.0)
            decay = jnp.asarray(alpha, dtype) ** exponent
            return jnp.where(causal, decay, jnp.zeros((), dtype))
        key = jax.random.key(seed)
        k1, k2, k3 = jax.random.split(key, 3)
        x = jax.random.normal(k1, (BATCH, MAX_LEN, EMBED_DIM), dtype=jnp.float32)
        scale = 1.0 / np.sqrt(EMBED_DIM)
        W_qkv = jax.random.uniform(k2, (EMBED_DIM, 3 * EMBED_DIM), dtype=jnp.float32, minval=-scale, maxval=scale)
        b_qkv = jax.random.uniform(k3, (3 * EMBED_DIM,), dtype=jnp.float32, minval=-scale, maxval=scale)
        return {'x': x, 'W_qkv': W_qkv, 'b_qkv': b_qkv}
    _L0_attn_all = _L0_attn_setup()
    _L0_attn_in = {k: v for k, v in _L0_attn_all.items() if k in ('W_qkv', 'b_qkv')}
    del _L0_attn_all

    def _L0_ffn_setup():
        import math
        import jax, jax.numpy as jnp
        import numpy as np
        B, L, D = (8, 1024, 192)
        E = 16
        TOP_K = 2
        F_EXP = 4 * D
        F_SH = F_EXP * 2 // 4
        key = jax.random.key(seed)
        ks = jax.random.split(key, 8)
        s = lambda fan_in: 1.0 / math.sqrt(fan_in)
        return {'hidden_states': jax.random.normal(ks[0], (B, L, D), jnp.float32), 'gate_weight': jax.random.uniform(ks[1], (E, D), jnp.float32, -s(D), s(D)), 'Wg': jax.random.uniform(ks[2], (E, F_EXP, D), jnp.float32, -s(D), s(D)), 'Wu': jax.random.uniform(ks[3], (E, F_EXP, D), jnp.float32, -s(D), s(D)), 'Wd': jax.random.uniform(ks[4], (E, D, F_EXP), jnp.float32, -s(F_EXP), s(F_EXP)), 'Ws_g': jax.random.uniform(ks[5], (F_SH, D), jnp.float32, -s(D), s(D)), 'Ws_u': jax.random.uniform(ks[6], (F_SH, D), jnp.float32, -s(D), s(D)), 'Ws_d': jax.random.uniform(ks[7], (D, F_SH), jnp.float32, -s(F_SH), s(F_SH))}
    _L0_ffn_all = _L0_ffn_setup()
    _L0_ffn_in = {k: v for k, v in _L0_ffn_all.items() if k in ('gate_weight', 'Wg', 'Wu', 'Wd', 'Ws_g', 'Ws_u', 'Ws_d')}
    del _L0_ffn_all

    def _L1_attn_setup():
        import jax, jax.numpy as jnp
        import numpy as np
        B, N, DIM, H = (8, 256, 192, 12)
        DH = DIM // H
        LATENT = 32
        EPS = 1e-05

        def _heads(t):
            b, n, _ = t.shape
            return t.reshape(b, n, H, DH).transpose(0, 2, 1, 3).reshape(b * H, n, DH)

        def _merge(t, b):
            _, n, dh = t.shape
            return t.reshape(b, H, n, dh).transpose(0, 2, 1, 3).reshape(b, n, H * dh)

        def _ln(v, g, bta):
            mu = v.mean(-1, keepdims=True)
            var = ((v - mu) ** 2).mean(-1, keepdims=True)
            return (v - mu) * jax.lax.rsqrt(var + EPS) * g + bta

        def _rope(t):
            n, dh = (t.shape[-2], t.shape[-1])
            inv = 1.0 / 10000.0 ** (jnp.arange(0, dh, 2, dtype=jnp.float32) / dh)
            f = jnp.arange(n, dtype=jnp.float32)[:, None] * inv[None, :]
            f = jnp.concatenate([f, f], -1)[None]
            x1, x2 = jnp.split(t, 2, -1)
            rot = jnp.concatenate([-x2, x1], -1)
            return t * jnp.cos(f) + rot * jnp.sin(f)
        key = jax.random.key(seed)
        ks = jax.random.split(key, 6)
        s = 0.02
        return {'x': jax.random.normal(ks[0], (B, N, DIM), jnp.float32), 'Wq': jax.random.normal(ks[1], (DIM, DIM), jnp.float32) * s, 'Wkv': jax.random.normal(ks[2], (DIM, DIM), jnp.float32) * s, 'Wo_ctx': jax.random.normal(ks[3], (DIM, DIM), jnp.float32) * s, 'bo_ctx': jnp.zeros((DIM,), jnp.float32), 'Wo_lat': jax.random.normal(ks[4], (DIM, DIM), jnp.float32) * s, 'bo_lat': jnp.zeros((DIM,), jnp.float32), 'ln_g': jnp.ones((DH,), jnp.float32), 'ln_b': jnp.zeros((DH,), jnp.float32)}
    _L1_attn_all = _L1_attn_setup()
    _L1_attn_in = {k: v for k, v in _L1_attn_all.items() if k in ('Wq', 'Wkv', 'Wo_ctx', 'bo_ctx', 'Wo_lat', 'bo_lat', 'ln_g', 'ln_b')}
    del _L1_attn_all

    def _L1_ffn_setup():
        import jax, jax.numpy as jnp
        import numpy as np
        B, S, D = (2, 512, 192)
        E, K, F = (8, 2, 384)

        def _swiglu(xf, wg, wu, wd):
            return jax.nn.silu(xf @ wg.T) * (xf @ wu.T) @ wd.T
        key = jax.random.key(seed)
        ks = jax.random.split(key, 9)
        scale = 0.02
        x = jax.random.normal(ks[0], (B, S, D), dtype=jnp.float32)
        w_router = jax.random.normal(ks[1], (E, D), dtype=jnp.float32) * scale
        expert_bias = jnp.zeros((E,), dtype=jnp.float32)
        Wg = jax.random.normal(ks[2], (E, F, D), dtype=jnp.float32) * scale
        Wu = jax.random.normal(ks[3], (E, F, D), dtype=jnp.float32) * scale
        Wd = jax.random.normal(ks[4], (E, D, F), dtype=jnp.float32) * scale
        sg = jax.random.normal(ks[5], (F, D), dtype=jnp.float32) * scale
        su = jax.random.normal(ks[6], (F, D), dtype=jnp.float32) * scale
        sd = jax.random.normal(ks[7], (D, F), dtype=jnp.float32) * scale
        return {'x': x, 'w_router': w_router, 'expert_bias': expert_bias, 'Wg': Wg, 'Wu': Wu, 'Wd': Wd, 'sg': sg, 'su': su, 'sd': sd}
    _L1_ffn_all = _L1_ffn_setup()
    _L1_ffn_in = {k: v for k, v in _L1_ffn_all.items() if k in ('w_router', 'expert_bias', 'Wg', 'Wu', 'Wd', 'sg', 'su', 'sd')}
    del _L1_ffn_all
    return {'x': x, 'cls_tok': cls_tok, 'L0_tok_W0': _L0_tok_in['W0'], 'L0_tok_b0': _L0_tok_in['b0'], 'L0_tok_W1': _L0_tok_in['W1'], 'L0_tok_b1': _L0_tok_in['b1'], 'L0_tok_W2': _L0_tok_in['W2'], 'L0_tok_b2': _L0_tok_in['b2'], 'L0_attn_W_qkv': _L0_attn_in['W_qkv'], 'L0_attn_b_qkv': _L0_attn_in['b_qkv'], 'L0_ffn_gate_weight': _L0_ffn_in['gate_weight'], 'L0_ffn_Wg': _L0_ffn_in['Wg'], 'L0_ffn_Wu': _L0_ffn_in['Wu'], 'L0_ffn_Wd': _L0_ffn_in['Wd'], 'L0_ffn_Ws_g': _L0_ffn_in['Ws_g'], 'L0_ffn_Ws_u': _L0_ffn_in['Ws_u'], 'L0_ffn_Ws_d': _L0_ffn_in['Ws_d'], 'L1_attn_Wq': _L1_attn_in['Wq'], 'L1_attn_Wkv': _L1_attn_in['Wkv'], 'L1_attn_Wo_ctx': _L1_attn_in['Wo_ctx'], 'L1_attn_bo_ctx': _L1_attn_in['bo_ctx'], 'L1_attn_Wo_lat': _L1_attn_in['Wo_lat'], 'L1_attn_bo_lat': _L1_attn_in['bo_lat'], 'L1_attn_ln_g': _L1_attn_in['ln_g'], 'L1_attn_ln_b': _L1_attn_in['ln_b'], 'L1_ffn_w_router': _L1_ffn_in['w_router'], 'L1_ffn_expert_bias': _L1_ffn_in['expert_bias'], 'L1_ffn_Wg': _L1_ffn_in['Wg'], 'L1_ffn_Wu': _L1_ffn_in['Wu'], 'L1_ffn_Wd': _L1_ffn_in['Wd'], 'L1_ffn_sg': _L1_ffn_in['sg'], 'L1_ffn_su': _L1_ffn_in['su'], 'L1_ffn_sd': _L1_ffn_in['sd']}

def reference(x, cls_tok, L0_tok_W0, L0_tok_b0, L0_tok_W1, L0_tok_b1, L0_tok_W2, L0_tok_b2, L0_attn_W_qkv, L0_attn_b_qkv, L0_ffn_gate_weight, L0_ffn_Wg, L0_ffn_Wu, L0_ffn_Wd, L0_ffn_Ws_g, L0_ffn_Ws_u, L0_ffn_Ws_d, L1_attn_Wq, L1_attn_Wkv, L1_attn_Wo_ctx, L1_attn_bo_ctx, L1_attn_Wo_lat, L1_attn_bo_lat, L1_attn_ln_g, L1_attn_ln_b, L1_ffn_w_router, L1_ffn_expert_bias, L1_ffn_Wg, L1_ffn_Wu, L1_ffn_Wd, L1_ffn_sg, L1_ffn_su, L1_ffn_sd):
    import jax
    import jax.numpy as jnp

    def _L0_tok_ref(images, W0, b0, W1, b1, W2, b2):
        import jax, jax.numpy as jnp
        import numpy as np
        PATCH_SIZES = (8, 16, 32)
        PROJ_DIM = 192
        C = 3

        def _extract_patches(images, p):
            B, H, W, Cc = images.shape
            nh, nw = (H // p, W // p)
            x = images.reshape(B, nh, p, nw, p, Cc)
            x = x.transpose(0, 1, 3, 2, 4, 5)
            return x.reshape(B, nh * nw, p * p * Cc)
        Ws = (W0, W1, W2)
        bs = (b0, b1, b2)
        outs = []
        for p, W, b in zip(PATCH_SIZES, Ws, bs):
            patches = _extract_patches(images, p)
            outs.append(jnp.einsum('bnk,kd->bnd', patches, W) + b)
        return jnp.concatenate(outs, axis=1)

    def _L0_attn_ref(x, W_qkv, b_qkv):
        import jax, jax.numpy as jnp
        import numpy as np
        EMBED_DIM = 192
        MAX_LEN = 256
        ALPHA = 0.99
        BATCH = 16

        def _retention_mask(sl, alpha, dtype):
            i = jnp.arange(sl)[:, None]
            j = jnp.arange(sl)[None, :]
            causal = i >= j
            exponent = jnp.where(causal, (i - j).astype(dtype), 0.0)
            decay = jnp.asarray(alpha, dtype) ** exponent
            return jnp.where(causal, decay, jnp.zeros((), dtype))
        bs, sl, d = x.shape
        qkv = x @ W_qkv + b_qkv
        q, k, v = jnp.split(qkv, 3, axis=-1)
        M = _retention_mask(sl, ALPHA, x.dtype)
        scores = jnp.einsum('bsd,btd->bst', q, k) / jnp.sqrt(jnp.asarray(d, x.dtype))
        out = jnp.einsum('bst,btd->bsd', scores * M[None, :, :], v)
        return out

    def _L0_ffn_ref(hidden_states, gate_weight, Wg, Wu, Wd, Ws_g, Ws_u, Ws_d):
        import math
        import jax, jax.numpy as jnp
        import numpy as np
        B, L, D = (8, 1024, 192)
        E = 16
        TOP_K = 2
        F_EXP = 4 * D
        F_SH = F_EXP * 2 // 4
        b, l, d = hidden_states.shape
        n = b * l
        x = hidden_states.reshape(n, d)
        scores = jax.nn.sigmoid(x @ gate_weight.T)
        capacity = math.ceil(n / E * TOP_K)
        topk_score, topk_ids = jax.lax.top_k(scores.T, capacity)
        xg = x[topk_ids]
        gate = jax.nn.silu(jnp.einsum('ecd,efd->ecf', xg, Wg))
        up = jnp.einsum('ecd,efd->ecf', xg, Wu)
        out = jnp.einsum('ecf,edf->ecd', gate * up, Wd)
        out = out * topk_score[..., None]
        y = jnp.zeros((n, d), x.dtype).at[topk_ids.reshape(-1)].add(out.reshape(-1, d))
        y = y.reshape(b, l, d)
        shared = jax.nn.silu(hidden_states @ Ws_g.T) * (hidden_states @ Ws_u.T) @ Ws_d.T
        return y + shared

    def _L1_attn_ref(x, Wq, Wkv, Wo_ctx, bo_ctx, Wo_lat, bo_lat, ln_g, ln_b):
        import jax, jax.numpy as jnp
        import numpy as np
        B, N, DIM, H = (8, 256, 192, 12)
        DH = DIM // H
        LATENT = 32
        EPS = 1e-05

        def _heads(t):
            b, n, _ = t.shape
            return t.reshape(b, n, H, DH).transpose(0, 2, 1, 3).reshape(b * H, n, DH)

        def _merge(t, b):
            _, n, dh = t.shape
            return t.reshape(b, H, n, dh).transpose(0, 2, 1, 3).reshape(b, n, H * dh)

        def _ln(v, g, bta):
            mu = v.mean(-1, keepdims=True)
            var = ((v - mu) ** 2).mean(-1, keepdims=True)
            return (v - mu) * jax.lax.rsqrt(var + EPS) * g + bta

        def _rope(t):
            n, dh = (t.shape[-2], t.shape[-1])
            inv = 1.0 / 10000.0 ** (jnp.arange(0, dh, 2, dtype=jnp.float32) / dh)
            f = jnp.arange(n, dtype=jnp.float32)[:, None] * inv[None, :]
            f = jnp.concatenate([f, f], -1)[None]
            x1, x2 = jnp.split(t, 2, -1)
            rot = jnp.concatenate([-x2, x1], -1)
            return t * jnp.cos(f) + rot * jnp.sin(f)
        b, n, _ = x.shape
        ctx = n - LATENT
        q = _heads(x @ Wq)
        kv = _heads(x @ Wkv)
        q = _rope(q)
        kv = _rope(kv)
        q = q * DH ** (-0.5)
        q_lat, q_ctx = (q[:, ctx:], q[:, :ctx])
        kv_ctx = kv[:, :ctx]
        lkv = _ln(kv, ln_g, ln_b)
        lkv_ctx = _ln(kv_ctx, ln_g, ln_b)
        attn_lat = jax.nn.softmax(jnp.einsum('bid,bkd->bik', q_lat, kv), axis=-1)
        attn_ctx = jax.nn.softmax(jnp.einsum('bid,bkd->bik', q_ctx, kv_ctx), axis=-1)
        out_lat = _merge(jnp.einsum('bik,bkd->bid', attn_lat, lkv), b) @ Wo_lat + bo_lat
        out_ctx = _merge(jnp.einsum('bik,bkd->bid', attn_ctx, lkv_ctx), b) @ Wo_ctx + bo_ctx
        return jnp.concatenate([out_ctx, out_lat], axis=1)

    def _L1_ffn_ref(x, w_router, expert_bias, Wg, Wu, Wd, sg, su, sd):
        import jax, jax.numpy as jnp
        import numpy as np
        B, S, D = (2, 512, 192)
        E, K, F = (8, 2, 384)

        def _swiglu(xf, wg, wu, wd):
            return jax.nn.silu(xf @ wg.T) * (xf @ wu.T) @ wd.T
        b, s, d = x.shape
        xf = x.reshape(-1, d)
        T = xf.shape[0]
        e = w_router.shape[0]
        logits = xf @ w_router.T
        scores = jax.nn.softmax(logits, axis=-1)
        selection = scores + expert_bias[None, :]
        _, top_idx = jax.lax.top_k(selection, K)
        top_s = jnp.take_along_axis(scores, top_idx, axis=-1)
        top_s = top_s / (jnp.sum(top_s, axis=-1, keepdims=True) + 1e-09)
        comb = jnp.zeros((T, e), dtype=x.dtype).at[jnp.arange(T)[:, None], top_idx].add(top_s)

        def body(acc, p):
            wg, wu, wd, c = p
            return (acc + c[:, None] * _swiglu(xf, wg, wu, wd), None)
        routed, _ = jax.lax.scan(body, jnp.zeros_like(xf), (Wg, Wu, Wd, comb.T))
        out = routed + _swiglu(xf, sg, su, sd)
        return out.reshape(b, s, d)
    h = _L0_tok_ref(x, L0_tok_W0, L0_tok_b0, L0_tok_W1, L0_tok_b1, L0_tok_W2, L0_tok_b2)
    h = jnp.concatenate([jnp.broadcast_to(cls_tok, (h.shape[0], 1, h.shape[2])), h], axis=1)
    h = h + _L0_attn_ref(_layernorm(h, axis=-1), L0_attn_W_qkv, L0_attn_b_qkv)
    h = h + _L0_ffn_ref(_layernorm(h, axis=-1), L0_ffn_gate_weight, L0_ffn_Wg, L0_ffn_Wu, L0_ffn_Wd, L0_ffn_Ws_g, L0_ffn_Ws_u, L0_ffn_Ws_d)
    h = h + _L1_attn_ref(_layernorm(h, axis=-1), L1_attn_Wq, L1_attn_Wkv, L1_attn_Wo_ctx, L1_attn_bo_ctx, L1_attn_Wo_lat, L1_attn_bo_lat, L1_attn_ln_g, L1_attn_ln_b)
    h = h + _L1_ffn_ref(_layernorm(h, axis=-1), L1_ffn_w_router, L1_ffn_expert_bias, L1_ffn_Wg, L1_ffn_Wu, L1_ffn_Wd, L1_ffn_sg, L1_ffn_su, L1_ffn_sd)
    return h

_drawn_inputs = setup_inputs


def setup_inputs(seed=0):
    import zlib

    import numpy as np

    out = dict(_drawn_inputs(seed))
    spreads = {'L0_tok_b0': (0.0, 0.1),
     'L0_tok_b1': (0.0, 0.1),
     'L0_tok_b2': (0.0, 0.1),
     'L1_attn_bo_ctx': (0.0, 0.1),
     'L1_attn_bo_lat': (0.0, 0.8),
     'L1_attn_ln_g': (1.0, 0.6),
     'L1_attn_ln_b': (0.0, 0.778),
     'L1_ffn_expert_bias': (0.0, 0.8)}
    factors = {'cls_tok': 2.759,
     'L1_attn_Wq': 8.0,
     'L1_attn_Wkv': 6.521,
     'L1_attn_Wo_ctx': 4.452,
     'L1_attn_Wo_lat': 8.0,
     'L1_ffn_w_router': 8.0,
     'L1_ffn_Wg': 8.0,
     'L1_ffn_Wu': 8.0,
     'L1_ffn_Wd': 8.0,
     'L1_ffn_sg': 8.0,
     'L1_ffn_su': 8.0,
     'L1_ffn_sd': 8.0}
    for name, (base, spread) in spreads.items():
        noise = np.random.default_rng([zlib.crc32(name.encode()), seed]).standard_normal(out[name].shape)
        drawn = base * np.exp(spread * noise) if base else spread * noise
        out[name] = jnp.asarray(drawn.astype(out[name].dtype))
    for name, factor in factors.items():
        out[name] = (out[name] * factor).astype(out[name].dtype)
    return out
```

```python
from contextlib import ExitStack

import numpy as np

import concourse.bass as bass
from concourse import mybir

F32 = mybir.dt.float32
BF16 = mybir.dt.bfloat16
I32 = mybir.dt.int32
U32 = mybir.dt.uint32
ALU = mybir.AluOpType
ACT = mybir.ActivationFunctionType
AX_X = mybir.AxisListType.X

B = 8
D = 192
DC, DP = 2, 96
SEQ = 1030
TOK = B * SEQ
T = 103
NC = SEQ // T
HB = B // 2
W4 = HB * T
EPS = 1e-5
ALPHA = float(np.float32(0.99))
PATCH = ((8, 784, 192), (16, 196, 768), (32, 49, 3072))

E0, F0, CAP = 16, 768, 1030
FS0 = 384
E1, F1 = 8, 384
HEADS, DH, LAT = 12, 16, 32
CTX = SEQ - LAT


def names(ctx, nc):
    sems = []

    def sb(name, shape, dt=F32):
        return ctx.enter_context(nc.sbuf_tensor(name, shape, dt))

    def sem(name):
        sems.append(nc.alloc_semaphore(name))
        return sems[-1]

    def clear():
        nc.clear_and_free_semaphores(sems)
        nc.all_engine_barrier()

    ctx.callback(clear)
    return sb, sem


def spread(row, partitions):
    return row.rearrange("(a n) -> a n", a=1).broadcast_to([partitions, row.shape[0]])


def phase_patches(nc, psum, inp, h0):
    with ExitStack() as ctx:
        sb, sem = names(ctx, nc)
        w8 = sb("tok_w8", [DP, 2, D])
        w16 = sb("tok_w16", [128, 6, D])
        w32 = sb("tok_w32", [128, 24, D])
        bias = sb("tok_bias", [128, 3, 2, D])
        cls = sb("tok_cls", [B, D])
        p8 = sb("tok_p8", [DP, 2, 2, 2, 784])
        p16 = sb("tok_p16", [128, 2, 6, 2, 196])
        p32 = sb("tok_p32", [128, 2, 24, 2, 49])
        o8 = sb("tok_o8", [112, 2, 2, 7, D])
        o16 = sb("tok_o16", [98, 2, 2, 2, D])
        o32 = sb("tok_o32", [98, 2, D])
        weights_in = sem("tok_weights_in")
        cls_in, cls_out = sem("tok_cls_in"), sem("tok_cls_out")
        patches_in = [sem("tok_patches_in0"), sem("tok_patches_in1")]
        patches_used = [sem("tok_patches_used0"), sem("tok_patches_used1")]
        bank_full = sem("tok_bank_full")
        rows_ready = sem("tok_rows_ready")
        rows_out = [sem("tok_rows_out0"), sem("tok_rows_out1")]
        PAIRS = B // 2

        h_img = h0.rearrange("(b n) d -> b n d", b=B)
        x8 = inp["x8"].rearrange("(c p) b n -> p c b n", c=2)
        x16 = inp["x16"].rearrange("(c p) b n -> p c b n", c=6)
        x32 = inp["x32"].rearrange("(c p) b n -> p c b n", c=24)

        JOBS = []
        for img in range(2):
            JOBS += [(0, img, (0, 1)), (0, img, (2, 3)), (0, img, (4, 5)), (0, img, (6,)), (1, img, (0, 1))]
        JOBS += [(2, 0, (0,))]
        NJ = len(JOBS)
        ROWS = (112, 98, 98)

        def filled(size, half, img, tiles):
            n = len(tiles)
            if size == 0:
                return o8[:, half, img, tiles[0]:tiles[0] + n, :]
            if size == 1:
                return o16[:, half, img, :, :]
            return o32[:, half, :].rearrange("p (a d) -> p a d", a=1)

        block = ctx.enter_context(nc.Block())

        @block.sync
        def _(sp):
            sp.dma_start(w8[:], inp["L0_tok_W0"].rearrange("(c p) d -> p c d", c=2)).then_inc(weights_in, 16)
            sp.dma_start(w16[:], inp["L0_tok_W1"].rearrange("(c p) d -> p c d", c=6)).then_inc(weights_in, 16)
            sp.dma_start(w32[:], inp["L0_tok_W2"].rearrange("(c p) d -> p c d", c=24)).then_inc(weights_in, 16)
            with sp.Fori(0, PAIRS // 2) as i:
                for half in range(2):
                    first = i * 4 + half * 2
                    sp.wait_ge(patches_used[half], i)
                    for c in range(2):
                        sp.dma_start(p8[:, half, c], x8[:, c, bass.ds(first, 2), :]).then_inc(patches_in[half], 16)
                    for img in range(2):
                        sp.dma_start(p16[:, half, :, img], x16[:, :, bass.ds(first + img, 1), :]
                                     .rearrange("p c b n -> p c (b n)")).then_inc(patches_in[half], 16)
                        sp.dma_start(p32[:, half, :, img], x32[:, :, bass.ds(first + img, 1), :]
                                     .rearrange("p c b n -> p c (b n)")).then_inc(patches_in[half], 16)

        @block.gpsimd
        def _(pool):
            pool.dma_start(cls[:], inp["cls_tok"].rearrange("a b d -> (a b) d").broadcast_to([B, D])).then_inc(cls_in, 16)
            pool.wait_ge(cls_in, 16)
            pool.dma_start(h_img[:, 0, :], cls[:]).then_inc(cls_out, 16)
            pool.wait_ge(cls_out, 16)

        @block.tensor
        def _(pe):
            pe.wait_ge(weights_in, 16 * 9)
            with pe.Fori(0, PAIRS // 2) as i:
                for half in range(2):
                    done = i * (2 * NJ) + half * NJ
                    pe.wait_ge(patches_in[half], i * 96 + 96)
                    pe.wait_ge(rows_ready, done)
                    for j, (size, img, tiles) in enumerate(JOBS):
                        if j >= 8:
                            pe.wait_ge(rows_ready, done + (j - 7))
                        for k, t in enumerate(tiles):
                            if size == 0:
                                parts = [(p8[:, half, c, img, 112 * t:112 * t + 112], w8[:, c, :]) for c in range(2)]
                            elif size == 1:
                                parts = [(p16[:, half, c, img, 98 * t:98 * t + 98], w16[:, c, :]) for c in range(6)]
                            else:
                                parts = [(p32[:, half, c, :, :], w32[:, c, :]) for c in range(24)]
                            for c, (lhs, rhs) in enumerate(parts):
                                last = pe.matmul(psum[0:ROWS[size], j % 8, k * D:(k + 1) * D], lhs, rhs,
                                                 start=(c == 0), stop=(c == len(parts) - 1))
                        last.then_inc(bank_full if j < NJ - 1 else patches_used[half], 1)

        @block.vector
        def _(dve):
            with dve.Fori(0, PAIRS // 2) as i:
                for half in range(2):
                    done = i * (2 * NJ) + half * NJ
                    dve.wait_ge(rows_out[half], i * 96)
                    for j, (size, img, tiles) in enumerate(JOBS):
                        if j < NJ - 1:
                            dve.wait_ge(bank_full, i * (2 * NJ - 2) + (half * (NJ - 1) + j + 1))
                        else:
                            dve.wait_ge(patches_used[half], i + 1)
                        n = len(tiles)
                        dve.tensor_tensor(filled(size, half, img, tiles),
                                          psum[0:ROWS[size], j % 8, 0:n * D].rearrange("p (a d) -> p a d", a=n),
                                          bias[0:ROWS[size], size, 0:n, :], ALU.add).then_inc(rows_ready, 1)

        @block.scalar
        def _(act):
            for size in range(3):
                for k in range(2):
                    act.dma_start(bias[:, size, k, :], spread(inp[f"L0_tok_b{size}"], 128)).then_inc(weights_in, 16)
            with act.Fori(0, PAIRS // 2) as i:
                for half in range(2):
                    done = i * (2 * NJ) + half * NJ
                    first = i * 4 + half * 2
                    for img in range(2):
                        rows = h_img[bass.ds(first + img, 1), :, :].rearrange("b n d -> (b n) d")
                        act.wait_ge(rows_ready, done + 5 * (img + 1))
                        act.dma_start(rows[1:785, :].rearrange("(t p) d -> p t d", t=7),
                                      o8[:, half, img]).then_inc(rows_out[half], 16)
                        act.dma_start(rows[785:981, :].rearrange("(t p) d -> p t d", t=2),
                                      o16[:, half, img]).then_inc(rows_out[half], 16)
                    act.wait_ge(rows_ready, done + NJ)
                    for img in range(2):
                        rows = h_img[bass.ds(first + img, 1), :, :].rearrange("b n d -> (b n) d")
                        act.dma_start(rows[981:1030, :], o32[49 * img:49 * img + 49, half, :]).then_inc(rows_out[half], 16)
            for half in range(2):
                act.wait_ge(rows_out[half], PAIRS // 2 * 96)


def phase_retention(nc, psum, inp, h0, h1, xg, x1T):
    with ExitStack() as ctx:
        sb, sem = names(ctx, nc)
        wqkv = sb("ret_wqkv", [DP, DC, 3 * D])
        bqk = sb("ret_bqk", [DP, 2, DC])
        brow = sb("ret_brow", [T, 2 * D])
        bkd = sb("ret_bkd", [T, D])
        dmask = sb("ret_dmask", [T, W4])
        qdec = sb("ret_qdec", [DP, W4])
        kdec = sb("ret_kdec", [T, 1])
        ident = sb("ret_ident", [128, 128])
        eps = sb("ret_eps", [128, 1])
        h_in = sb("ret_h_in", [T, 2, B, D])
        xn = sb("ret_xn", [T, B, D])
        xnT = sb("ret_xnT", [DP, DC, B * T])
        qT = sb("ret_qT", [DP, DC, B * T])
        qsT = sb("ret_qsT", [DP, DC, B * T])
        kT = sb("ret_kT", [DP, DC, B * T])
        kd = sb("ret_kd", [T, B, D])
        v = sb("ret_v", [T, B, D])
        pT = sb("ret_pT", [T, B * T])
        state = sb("ret_state", [DP, B, DC, D])
        h_out = sb("ret_h_out", [T, B, D])
        x_out = sb("ret_x_out", [T, B, D])
        stats = sb("ret_stats", [T, 2, B, 6])
        mv = sb("ret_mv", [T, 2, B, 2])
        std = sb("ret_std", [T, 2, B])
        pad = sb("ret_pad", [T, 1])
        rstd = sb("ret_rstd", [T, 2, B])

        consts_in = sem("ret_consts_in")
        eps_set = sem("ret_eps_set")
        bkd_ready = sem("ret_bkd_ready")
        state_zero = sem("ret_state_zero")
        h_loaded = [sem("ret_h_loaded0"), sem("ret_h_loaded1")]
        stats_ready = [sem(f"ret_stats_ready{k}") for k in range(2)]
        moments_ready = [sem(f"ret_moments_ready{k}") for k in range(2)]
        std_ready = [sem(f"ret_std_ready{k}") for k in range(2)]
        rstd_ready = [sem(f"ret_rstd_ready{k}") for k in range(2)]
        xn_ready = sem("ret_xn_ready")
        xnT_full = sem("ret_xnT_full")
        xnT_ready = sem("ret_xnT_ready")
        q_full, q_ready, qs_ready = sem("ret_q_full"), sem("ret_q_ready"), sem("ret_qs_ready")
        k_full, k_ready = sem("ret_k_full"), sem("ret_k_ready")
        kv_full, kv_ready = sem("ret_kv_full"), sem("ret_kv_ready")
        s_full, p_ready = sem("ret_s_full"), sem("ret_p_ready")
        o_full, h_ready = sem("ret_o_full"), sem("ret_h_ready")
        st_full, st_ready = sem("ret_st_full"), sem("ret_st_ready")
        x_ready = sem("ret_x_ready")
        xT_full, xT_ready = sem("ret_xT_full"), sem("ret_xT_ready")
        h_stored, x_stored = sem("ret_h_stored"), sem("ret_x_stored")

        def chunk_rows(dram, c, width):
            return dram.rearrange("(b c p) d -> c p b d", b=B, c=NC)[bass.ds(c, 1), :, :, 0:width] \
                .rearrange("c p b d -> p (c b) d")

        def bank(k, rows, width):
            return psum[0:rows, k, 0:width]

        block = ctx.enter_context(nc.Block())

        @block.sync
        def _(sp):
            sp.dma_start(wqkv[:], inp["L0_attn_W_qkv"].rearrange("(c p) n -> p c n", c=DC)).then_inc(consts_in, 16)
            sp.dma_start(dmask[:], inp["ret_dmask"]).then_inc(consts_in, 16)
            sp.dma_start(qdec[:], inp["ret_qdec"]).then_inc(consts_in, 16)
            sp.dma_start(kdec[:], inp["ret_kdec"]).then_inc(consts_in, 16)
            sp.dma_start(ident[:], inp["ident"]).then_inc(consts_in, 16)
            sp.dma_start(brow[:], spread(inp["L0_attn_b_qkv"][D:3 * D], T)).then_inc(consts_in, 16)
            with nc.allow_non_contiguous_dma(reason="two small biases, features to partitions"):
                for n in range(2):
                    sp.dma_start(bqk[:, n, :], inp["L0_attn_b_qkv"][n * D:n * D + D].rearrange("(c p) -> p c", c=DC)) \
                        .then_inc(consts_in, 16)
            for half in range(2):
                sp.dma_start(h_in[:, half], chunk_rows(h0, half, D)).then_inc(h_loaded[half], 16)

            def store(c):
                sp.wait_ge(h_ready, c * 4 + 4)
                sp.dma_start(chunk_rows(h1, c, D), h_out[:]).then_inc(h_stored, 16)
                sp.wait_ge(x_ready, c * 8 + 8)
                sp.dma_start(chunk_rows(xg, c, D), x_out[:]).then_inc(x_stored, 16)

            with sp.Fori(0, NC // 2 - 1) as i:
                for half in range(2):
                    c = i * 2 + half
                    sp.wait_ge(h_ready, c * 4 + 4)
                    sp.dma_start(h_in[:, half], chunk_rows(h0, c + 2, D)).then_inc(h_loaded[half], 16)
                    store(c)
            for c in (NC - 2, NC - 1):
                store(c)
            sp.wait_ge(h_stored, 16 * NC)
            sp.wait_ge(x_stored, 16 * NC)

        @block.gpsimd
        def _(pool):
            pool.memset(eps[:], EPS).then_inc(eps_set, 1)
            pool.memset(state[:], 0.0).then_inc(state_zero, 1)
            pool.wait_ge(consts_in, 16 * 8)
            with pool.Fori(0, NC) as c:
                for g in range(2):
                    for m in range(DC):
                        pool.wait_ge(q_ready, c * 4 + (2 * g + m + 1))
                        pool.wait_ge(o_full, c * 4)
                        pool.tensor_tensor(qsT[:, m, g * W4:(g + 1) * W4], qT[:, m, g * W4:(g + 1) * W4],
                                           qdec[:], ALU.mult).then_inc(qs_ready, 1)

        @block.tensor
        def _(pe):
            pe.wait_ge(consts_in, 16 * 8)
            pe.wait_ge(state_zero, 1)

            def turn_x1(c):
                for g in range(2):
                    pe.wait_ge(x_ready, c * 8 + (4 * g + 4))
                    for m in range(DC):
                        for b in range(HB):
                            last = pe.transpose(psum[0:DP, 2 * g + m, b * T:(b + 1) * T],
                                                x_out[:, g * HB + b, m * DP:(m + 1) * DP], ident[0:T, 0:T])
                        last.then_inc(xT_full, 1)

            def chunk(c, after_first):
                pe.wait_ge(h_ready, c * 4)
                for g in range(2):
                    pe.wait_ge(xn_ready, c * 8 + (4 * g + 4))
                    for m in range(DC):
                        for b in range(HB):
                            last = pe.transpose(psum[0:DP, 2 * g + m, b * T:(b + 1) * T],
                                                xn[:, g * HB + b, m * DP:(m + 1) * DP], ident[0:T, 0:T])
                        last.then_inc(xnT_full, 1)
                pe.wait_ge(st_ready, c * 8)
                for g in range(2):
                    pe.wait_ge(xnT_ready, c * 4 + (2 * g + 2))
                    for m in range(DC):
                        for k in range(DC):
                            last = pe.matmul(bank(4 + 2 * g + m, DP, W4), wqkv[:, k, m * DP:(m + 1) * DP],
                                             xnT[:, k, g * W4:(g + 1) * W4], start=(k == 0), stop=(k == 1))
                        last.then_inc(q_full, 1)
                if after_first:
                    turn_x1(c - 1)
                pe.wait_ge(xT_ready, c * 4)
                for g in range(2):
                    for m in range(DC):
                        for k in range(DC):
                            last = pe.matmul(bank(2 * g + m, DP, W4), wqkv[:, k, D + m * DP:D + (m + 1) * DP],
                                             xnT[:, k, g * W4:(g + 1) * W4], start=(k == 0), stop=(k == 1))
                        last.then_inc(k_full, 1)
                for b in range(B):
                    if b < 4:
                        pe.wait_ge(q_ready, c * 4 + (b + 1))
                    else:
                        pe.wait_ge(kv_ready, c * 8 + (b - 3))
                    for k in range(DC):
                        last = pe.matmul(bank(4 + b % 4, T, 2 * D), xnT[:, k, b * T:(b + 1) * T],
                                         wqkv[:, k, D:3 * D], start=(k == 0), stop=(k == 1))
                    last.then_inc(kv_full, 1)
                pe.wait_ge(k_ready, c * 4 + 4)
                for g in range(2):
                    for b in range(HB):
                        at = slice((g * HB + b) * T, (g * HB + b + 1) * T)
                        for k in range(DC):
                            last = pe.matmul(psum[0:T, g, b * T:(b + 1) * T], kT[:, k, at], qT[:, k, at],
                                             start=(k == 0), stop=(k == 1))
                    last.then_inc(s_full, 1)
                pe.wait_ge(qs_ready, c * 4 + 4)
                pe.wait_ge(kv_ready, c * 8 + 8)
                pe.wait_ge(st_ready, c * 8)
                for p in range(4):
                    pe.wait_ge(p_ready, c * 2 + (1 if p < 2 else 2))
                    for b in (2 * p, 2 * p + 1):
                        at = slice(b * T, (b + 1) * T)
                        o = psum[0:T, (2, 3, 0, 1)[p], (b % 2) * D:(b % 2 + 1) * D]
                        pe.matmul(o, pT[:, at], v[:, b, :], start=True, stop=False)
                        for k in range(DC):
                            last = pe.matmul(o, qsT[:, k, at], state[:, b, k, :], start=False, stop=(k == 1))
                    last.then_inc(o_full, 1)
                for b in range(B):
                    if b >= 4:
                        pe.wait_ge(st_ready, c * 8 + (b - 3))
                    for k in range(DC):
                        last = pe.matmul(psum[0:DP, 4 + b % 4, k * D:(k + 1) * D], kd[:, b, k * DP:(k + 1) * DP],
                                         v[:, b, :], start=True, stop=True)
                    last.then_inc(st_full, 1)

            chunk(0, False)
            with pe.Fori(1, NC) as c:
                chunk(c, True)
            pe.wait_ge(h_ready, NC * 4)
            turn_x1(NC - 1)

        @block.scalar
        def _(act):
            act.wait_ge(eps_set, 1)
            act.wait_ge(consts_in, 16 * 8)

            def root(n, c):
                act.wait_ge(moments_ready[n], c + 1)
                act.activation(std[:, n, :], mv[:, n, :, 1], ACT.Sqrt, bias=eps[0:T, :]).then_inc(std_ready[n], 1)

            def x1_out(c):
                for g in range(2):
                    for m in range(DC):
                        act.wait_ge(xT_full, c * 4 + (2 * g + m + 1))
                        act.activation(x1T[:, m, g * HB:(g + 1) * HB, bass.ds(c * T, T)],
                                       bank(2 * g + m, DP, W4).rearrange("p (b t) -> p b t", b=HB),
                                       ACT.Identity).then_inc(xT_ready, 1)

            def chunk(c, after_first, before_last):
                act.wait_ge(s_full, c * 2)
                act.wait_ge(qs_ready, c * 4)
                for g in range(2):
                    for m in range(DC):
                        act.wait_ge(q_full, c * 4 + (2 * g + m + 1))
                        act.activation(qT[:, m, g * W4:(g + 1) * W4], bank(4 + 2 * g + m, DP, W4), ACT.Identity,
                                       bias=bqk[:, 0, m:m + 1]).then_inc(q_ready, 1)
                if after_first:
                    x1_out(c - 1)
                if before_last:
                    root(0, c + 1)
                for g in range(2):
                    for m in range(DC):
                        act.wait_ge(k_full, c * 4 + (2 * g + m + 1))
                        act.activation(kT[:, m, g * W4:(g + 1) * W4], bank(2 * g + m, DP, W4), ACT.Identity,
                                       bias=bqk[:, 1, m:m + 1]).then_inc(k_ready, 1)
                root(1, c)

            root(0, 0)
            chunk(0, False, True)
            with act.Fori(1, NC - 1) as c:
                chunk(c, True, True)
            chunk(NC - 1, True, False)
            x1_out(NC - 1)

        @block.vector
        def _(dve):
            dve.wait_ge(consts_in, 16 * 8)
            dve.tensor_scalar(bkd[:], brow[:, 0:D], kdec[:, 0:1], None, ALU.mult).then_inc(bkd_ready, 1)
            dve.wait_ge(bkd_ready, 1)
            dve.wait_ge(state_zero, 1)

            def layernorm(n, c, rows, out, ready):
                for b in range(B):
                    last = dve.bn_stats(stats[:, n, b, :], rows[:, b, :])
                last.then_inc(stats_ready[n], 1)
                dve.wait_ge(stats_ready[n], c + 1)
                dve.memset(pad[:], 0.0)
                for b in range(B):
                    last = dve.bn_aggr(mv[:, n, b, :], stats[:, n, b, :])
                last.then_inc(moments_ready[n], 1)
                dve.wait_ge(std_ready[n], c + 1)
                dve.reciprocal(rstd[:, n, :], std[:, n, :]).then_inc(rstd_ready[n], 1)
                dve.wait_ge(rstd_ready[n], c + 1)
                for b in range(B):
                    dve.tensor_scalar(out[:, b, :], rows[:, b, :], mv[:, n, b, 0:1], rstd[:, n, b:b + 1],
                                      ALU.subtract, ALU.mult).then_inc(ready, 1)

            def take_xnT(c):
                dve.wait_ge(kv_full, c * 8)
                for g in range(2):
                    for m in range(DC):
                        dve.wait_ge(xnT_full, c * 4 + (2 * g + m + 1))
                        dve.tensor_copy(xnT[:, m, g * W4:(g + 1) * W4], bank(2 * g + m, DP, W4)) \
                            .then_inc(xnT_ready, 1)

            def chunk(c, i, half, before_last):
                if before_last:
                    dve.wait_ge(h_loaded[1 - half], i * 16 + 16 * (1 + half))
                    dve.wait_ge(xnT_full, c * 4 + 4)
                    layernorm(0, c + 1, h_in[:, 1 - half], xn, xn_ready)
                dve.wait_ge(st_full, c * 8)
                for b in range(B):
                    dve.wait_ge(kv_full, c * 8 + (b + 1))
                    dve.scalar_tensor_tensor(out=kd[:, b, :], in0=psum[0:T, 4 + b % 4, 0:D], scalar=kdec[:, 0:1],
                                             in1=bkd[:], op0=ALU.mult, op1=ALU.add)
                    dve.tensor_tensor(v[:, b, :], psum[0:T, 4 + b % 4, D:2 * D], brow[:, D:2 * D],
                                      ALU.add).then_inc(kv_ready, 1)
                dve.wait_ge(o_full, c * 4)
                for g in range(2):
                    dve.wait_ge(s_full, c * 2 + (g + 1))
                    dve.tensor_tensor(pT[:, g * W4:(g + 1) * W4], bank(g, T, W4), dmask[:], ALU.mult) \
                        .then_inc(p_ready, 1)
                dve.wait_ge(h_stored, c * 16)
                dve.wait_ge(x_ready, c * 8)
                for p in range(4):
                    dve.wait_ge(o_full, c * 4 + (p + 1))
                    dve.tensor_tensor(h_out[:, 2 * p:2 * p + 2, :],
                                      bank((2, 3, 0, 1)[p], T, 2 * D).rearrange("p (b d) -> p b d", b=2),
                                      h_in[:, half, 2 * p:2 * p + 2, :], ALU.add).then_inc(h_ready, 1)
                for b in range(B):
                    dve.wait_ge(st_full, c * 8 + (b + 1))
                    dve.scalar_tensor_tensor(out=state[:, b, :, :], in0=state[:, b, :, :], scalar=ALPHA ** T,
                                             in1=bank(4 + b % 4, DP, 2 * D).rearrange("p (c d) -> p c d", c=DC),
                                             op0=ALU.mult, op1=ALU.add).then_inc(st_ready, 1)
                if before_last:
                    take_xnT(c + 1)
                dve.wait_ge(x_stored, c * 16)
                dve.wait_ge(xT_full, c * 4)
                dve.wait_ge(h_ready, c * 4 + 4)
                layernorm(1, c, h_out, x_out, x_ready)

            dve.wait_ge(h_loaded[0], 16)
            layernorm(0, 0, h_in[:, 0], xn, xn_ready)
            take_xnT(0)
            with dve.Fori(0, NC // 2 - 1) as i:
                for half in range(2):
                    chunk(i * 2 + half, i, half, True)
            chunk(NC - 2, NC // 2 - 1, 0, True)
            chunk(NC - 1, NC // 2 - 1, 1, False)


def phase_route(nc, psum, inp, h1, xg, x1T, y, ids):
    BITS, STEPS = 30, 3
    LOOPS = BITS // STEPS
    FC = FS0 // 128
    GT = W4 // T
    ROUND = 1.5 * 2.0 ** 23
    assert 2 * LOOPS * W4 == TOK and NC == LOOPS
    with ExitStack() as ctx:
        sb, sem = names(ctx, nc)
        gate = sb("rt_gate", [DP, DC, E0])
        gpad = sb("rt_gpad", [DP, DC, B, 128])
        same = sb("rt_same", [128, 128])
        before = sb("rt_before", [128, 128])
        ident = sb("rt_ident", [128, 128])
        iota_lo = sb("rt_iota_lo", [T, T], BF16)
        iota_hi = sb("rt_iota_hi", [T, NC], BF16)
        tile0 = sb("rt_tile0", [T, 128], BF16)
        row = sb("rt_row", [T, 1])
        consts32 = sb("rt_consts32", [T, T + NC + 128])
        ones = sb("rt_ones", [128, SEQ])
        score = sb("rt_score", [128, SEQ])
        above = sb("rt_above", [128, SEQ])
        equal = sb("rt_equal", [128, SEQ])
        rank = sb("rt_rank", [128, SEQ])
        take = sb("rt_take", [128, SEQ])
        hi = sb("rt_hi", [128, SEQ])
        lo = sb("rt_lo", [128, SEQ])
        junk = sb("rt_junk", [128, SEQ], BF16)
        th = sb("rt_th", [128, 1], I32)
        cand = sb("rt_cand", [128, 1], I32)
        keep = sb("rt_keep", [128, 1], I32)
        bit = sb("rt_bit", [128, 1], I32)
        bitf = sb("rt_bitf", [128, 1])
        count = sb("rt_count", [128, 1])
        small = sb("rt_small", [128, 8])
        hiT = sb("rt_hiT", [T, NC, 128], BF16)
        loT = sb("rt_loT", [T, NC, 128], BF16)
        scT = sb("rt_scT", [T, NC, 128])
        hot_lo = sb("rt_hot_lo", [T, 128, T], BF16)
        hit = sb("rt_hit", [T, 128, NC], BF16)
        hot_hi = sb("rt_hot_hi", [T, 128, 2 * NC], BF16)
        zero = sb("rt_zero", [128, W4], BF16)
        idp = sb("rt_idp", [128, W4])
        idT = sb("rt_idT", [T, 4, 128])
        wg = sb("sh_wg", [DP, DC, FS0])
        wu = sb("sh_wu", [DP, DC, FS0])
        wd = sb("sh_wd", [128, FC, D])
        silu = sb("sh_silu", [128, 2, W4])
        hT = sb("sh_hT", [128, FC, W4])
        h_in = sb("sh_h_in", [T, GT, D])
        y_out = sb("sh_y_out", [T, GT, D])

        consts_in, consts_ready = sem("rt_consts_in"), sem("rt_consts_ready")
        zeroed = sem("rt_zeroed")
        gpad_ready, logits_full, score_ready = sem("rt_gpad_ready"), sem("rt_logits_full"), sem("rt_score_ready")
        cand_ready, counted, totalled = sem("rt_cand_ready"), sem("rt_counted"), sem("rt_totalled")
        keep_ready, th_ready, bit_ready = sem("rt_keep_ready"), sem("rt_th_ready"), sem("rt_bit_ready")
        step = sem("rt_step")
        sums_full = sem("rt_sums_full")
        turned, turned_out = sem("rt_turned"), sem("rt_turned_out")
        hit_ready, hot_ready, hot_used = sem("rt_hit_ready"), sem("rt_hot_ready"), sem("rt_hot_used")
        ids_open, ids_full, idp_ready = sem("rt_ids_open"), sem("rt_ids_full"), sem("rt_idp_ready")
        idT_full, idT_ready, ids_ready = sem("rt_idT_full"), sem("rt_idT_ready"), sem("rt_ids_ready")
        scores_out = sem("rt_scores_out")
        g_full, u_full = sem("sh_g_full"), sem("sh_u_full")
        silu_ready, hT_ready = sem("sh_silu_ready"), sem("sh_hT_ready")
        d_full, y_ready = sem("sh_d_full"), sem("sh_y_ready")
        h_loaded, y_stored = sem("sh_h_loaded"), sem("sh_y_stored")

        x_flat = x1T.rearrange("p c b n -> p c (b n)")
        h_tiles = h1.rearrange("(n k p) d -> n p k d", k=GT, p=T)
        y_tiles = y.rearrange("(n k p) d -> n p k d", k=GT, p=T)
        TOTAL = psum[:, 6, 0:1]
        LISTS = psum[:, 6, 0:W4]

        block = ctx.enter_context(nc.Block())

        @block.sync
        def _(sp):
            for dst, src in ((gate[:], inp["gateT"].rearrange("(c p) e -> p c e", c=DC)),
                             (same[:], inp["rt_same"]), (before[:], inp["rt_before"]), (ident[:], inp["ident"]),
                             (consts32[:], inp["rt_iota"]), (row[:], inp["rt_row"]),
                             (wg[:], inp["sh_gT"].rearrange("(c p) f -> p c f", c=DC)),
                             (wu[:], inp["sh_uT"].rearrange("(c p) f -> p c f", c=DC)),
                             (wd[:], inp["sh_dT"].rearrange("(c p) d -> p c d", c=FC))):
                sp.dma_start(dst, src).then_inc(consts_in, 16)
            with sp.Fori(0, 2 * LOOPS) as j:
                sp.wait_ge(y_ready, j * 2)
                sp.dma_start(h_in[:], h_tiles[bass.ds(j, 1)].rearrange("n p k d -> p (n k) d")).then_inc(h_loaded, 16)
                sp.wait_ge(y_ready, j * 2 + 2)
                sp.dma_start(y_tiles[bass.ds(j, 1)].rearrange("n p k d -> p (n k) d"), y_out[:]).then_inc(y_stored, 16)
            sp.wait_ge(y_stored, 16 * 2 * LOOPS)

        @block.gpsimd
        def _(pool):
            pool.memset(gpad[:], 0.0).then_inc(zeroed, 1)
            pool.memset(ones[:], 1.0).then_inc(zeroed, 1)
            pool.memset(zero[:], 0.0).then_inc(zeroed, 1)
            pool.wait_ge(turned_out, 9)
            rows = xg.rearrange("(b c p) d -> p c b d", b=B, c=NC)
            for c in range(NC):
                pool.dma_start(rows[:, c, :, D:D + E0], scT[:, c, :].rearrange("p (b e) -> p b e", b=B)) \
                    .then_inc(scores_out, 16)
            pool.wait_ge(scores_out, 16 * NC)

        def shared_up(pe, j, slices=range(FC)):
            for f in slices:
                pe.wait_ge(hT_ready, j * FC + max(f - 1, 0)) if f else pe.wait_ge(hT_ready, j * FC)
                for w, n, full in ((wg, 0, g_full), (wu, 1, u_full)):
                    for k in range(DC):
                        last = pe.matmul(psum[:, 2 * (f % 2) + n, 0:W4], w[:, k, f * 128:(f + 1) * 128],
                                         x_flat[:, k, bass.ds(j * W4, W4)], start=(k == 0), stop=(k == 1))
                    last.then_inc(full, 1)

        def shared_down(pe, j, halves=range(2)):
            pe.wait_ge(hT_ready, j * FC + FC)
            pe.wait_ge(y_ready, j * 2)
            for t in [2 * h + k for h in halves for k in range(2)]:
                for f in range(FC):
                    last = pe.matmul(psum[0:T, 4 + t // 2, (t % 2) * D:(t % 2 + 1) * D],
                                     hT[:, f, t * T:(t + 1) * T], wd[:, f, :], start=(f == 0), stop=(f == FC - 1))
                if t % 2:
                    last.then_inc(d_full, 1)

        @block.tensor
        def _(pe):
            pe.wait_ge(consts_in, 16 * 9)
            pe.wait_ge(gpad_ready, 1)
            for s, n in enumerate((W4, W4, SEQ - 2 * W4)):
                for b in range(B):
                    for k in range(DC):
                        last = pe.matmul(psum[:, s, 0:n], gpad[:, k, b, :], x1T[:, k, b, s * W4:s * W4 + n],
                                         start=(b == 0 and k == 0), stop=(b == B - 1 and k == 1))
                last.then_inc(logits_full, 1)
            pe.wait_ge(score_ready, 3)
            with pe.Fori(0, LOOPS) as j:
                def total(s):
                    pe.wait_ge(counted, j * STEPS + (s + 1))
                    pe.wait_ge(keep_ready, j * STEPS + s)
                    pe.matmul(TOTAL, same[:], count[:], start=True, stop=True).then_inc(totalled, 1)
                shared_up(pe, j, (0,))
                total(0)
                shared_up(pe, j, (1,))
                total(1)
                shared_up(pe, j, (2,))
                shared_down(pe, j, (0,))
                total(2)
                shared_down(pe, j, (1,))

            def sums(n, weights, rhs, bank):
                pe.wait_ge(step, n)
                pe.matmul(psum[:, bank, 0:1], weights[:], rhs, start=True, stop=True).then_inc(sums_full, 1)

            sums(1, same, small[:, 0:1], 6)
            sums(3, before, rank[:, SEQ - 1:SEQ], 7)
            sums(7, before, rank[:, SEQ - 1:SEQ], 5)
            pe.wait_ge(step, 12)
            for n, src in enumerate((hi, lo, score)):
                for s, c0 in enumerate(range(0, NC, 4)):
                    if 3 * n + s >= 3:
                        pe.wait_ge(turned_out, 3 * n + s - 2)
                    for c in range(c0, min(c0 + 4, NC)):
                        last = pe.transpose(psum[0:T, s, (c - c0) * 128:(c - c0 + 1) * 128],
                                            src[:, c * T:(c + 1) * T], ident[:])
                    last.then_inc(turned, 1)
            pe.matmul(LISTS, zero[:, 0:128], zero[:], start=True, stop=False, skip_group_check=True)
            pe.wait_ge(turned_out, 9)
            with pe.Fori(0, NC) as c:
                j = c + LOOPS
                shared_up(pe, j)
                shared_down(pe, j)
                pe.wait_ge(hot_ready, c + 1)
                for b in range(B):
                    for e in range(E0):
                        q, g = e % 4, e // 4
                        last = pe.matmul(psum[32 * q:32 * q + 2 * NC, 6, g * T:(g + 1) * T],
                                         hot_hi[:, b * E0 + e, :], hot_lo[:, b * E0 + e, :],
                                         start=False, stop=False, skip_group_check=True)
                last.then_inc(hot_used, 1)
            pe.matmul(LISTS, zero[:, 0:128], zero[:], start=False, stop=True, skip_group_check=True).then_inc(ids_full, 1)
            pe.wait_ge(idp_ready, 1)
            for g in range(4):
                last = pe.transpose(psum[0:T, 7, g * 128:(g + 1) * 128], idp[:, g * T:(g + 1) * T], ident[:])
            last.then_inc(idT_full, 1)

        def shared_silu(act, j):
            for f in range(FC):
                act.wait_ge(g_full, j * FC + (f + 1))
                act.wait_ge(hT_ready, j * FC + (f - 1)) if f else act.wait_ge(hT_ready, j * FC)
                act.activation(silu[:, f % 2, :], psum[:, 2 * (f % 2), 0:W4], ACT.Silu).then_inc(silu_ready, 1)

        @block.scalar
        def _(act):
            for s, n in enumerate((W4, W4, SEQ - 2 * W4)):
                act.wait_ge(logits_full, s + 1)
                act.activation(score[:, s * W4:s * W4 + n], psum[:, s, 0:n], ACT.Sigmoid).then_inc(score_ready, 1)
            with act.Fori(0, LOOPS) as j:
                shared_silu(act, j)
            for n, dst in enumerate((hiT, loT, scT)):
                for s, c0 in enumerate(range(0, NC, 4)):
                    w = min(4, NC - c0)
                    act.wait_ge(turned, 3 * n + s + 1)
                    act.activation(dst[:, c0:c0 + w, :], psum[0:T, s, 0:w * 128].rearrange("p (c n) -> p c n", c=w),
                                   ACT.Identity).then_inc(turned_out, 1)
            with act.Fori(0, NC) as c:
                shared_silu(act, c + LOOPS)

        def shared_mult(dve, j, slices=range(FC)):
            dve.wait_ge(d_full, j * 2)
            for f in slices:
                dve.wait_ge(silu_ready, j * FC + (f + 1))
                dve.wait_ge(u_full, j * FC + (f + 1))
                dve.tensor_tensor(hT[:, f, :], silu[:, f % 2, :], psum[:, 2 * (f % 2) + 1, 0:W4],
                                  ALU.mult).then_inc(hT_ready, 1)

        def shared_rows(dve, j):
            dve.wait_ge(h_loaded, j * 16 + 16)
            dve.wait_ge(y_stored, j * 16)
            for k in range(2):
                dve.wait_ge(d_full, j * 2 + (k + 1))
                dve.tensor_tensor(y_out[:, 2 * k:2 * k + 2, :],
                                  psum[0:T, 4 + k, 0:2 * D].rearrange("p (b d) -> p b d", b=2),
                                  h_in[:, 2 * k:2 * k + 2, :], ALU.add).then_inc(y_ready, 1)

        @block.vector
        def _(dve):
            dve.memset(th[:], 0)
            dve.memset(bit[:], 1 << (BITS - 1))
            dve.memset(bitf[:], 2.0 ** (BITS - 1)).then_inc(bit_ready, 1)
            dve.wait_ge(zeroed, 3)
            dve.wait_ge(consts_in, 16 * 9)
            for b in range(B):
                last = dve.tensor_copy(gpad[:, :, b, b * E0:(b + 1) * E0], gate[:])
            last.then_inc(gpad_ready, 1)
            dve.tensor_copy(iota_lo[:], consts32[:, 0:T])
            dve.tensor_copy(iota_hi[:], consts32[:, T:T + NC])
            dve.tensor_copy(tile0[:], consts32[:, T + NC:]).then_inc(consts_ready, 1)
            dve.wait_ge(score_ready, 3)
            with dve.Fori(0, LOOPS) as j:
                def try_bit(s):
                    n = j * STEPS + s
                    dve.wait_ge(bit_ready, n + 1)
                    dve.tensor_tensor(cand[:], th[:], bit[:], ALU.bitwise_or).then_inc(cand_ready, 1)
                    dve.wait_ge(cand_ready, n + 1)
                    dve.wait_ge(totalled, n)
                    dve.tensor_scalar(junk[:], score[:], cand[:].bitcast(F32), None, ALU.is_ge, ALU.add,
                                      accum_out=count[:]).then_inc(counted, 1)

                def keep_bit(s):
                    n = j * STEPS + s
                    dve.wait_ge(totalled, n + 1)
                    dve.tensor_scalar(keep[:], TOTAL, float(CAP), bitf[:, 0:1], ALU.is_ge, ALU.mult).then_inc(keep_ready, 1)
                    dve.wait_ge(keep_ready, n + 1)
                    dve.tensor_tensor(th[:], th[:], keep[:], ALU.bitwise_or).then_inc(th_ready, 1)
                    dve.tensor_scalar(bitf[:], bitf[:], 0.5, None, ALU.mult)
                    dve.tensor_scalar(bit[:], bit[:], 1, None, ALU.logical_shift_right).then_inc(bit_ready, 1)
                try_bit(0)
                shared_mult(dve, j, (0,))
                keep_bit(0)
                try_bit(1)
                shared_mult(dve, j, (1,))
                keep_bit(1)
                try_bit(2)
                shared_mult(dve, j, (2,))
                keep_bit(2)
                shared_rows(dve, j)
            thf = th[:].bitcast(F32)
            dve.wait_ge(th_ready, BITS)
            n_above, need, off_equal, off_take = (small[:, k:k + 1] for k in range(4))
            dve.tensor_scalar(above[:], score[:], thf, None, ALU.is_gt, ALU.add, accum_out=n_above).then_inc(step, 1)
            dve.tensor_scalar(equal[:], score[:], thf, None, ALU.is_equal).then_inc(step, 1)
            dve.wait_ge(step, 2)
            dve.tensor_tensor_scan(rank[:], ones[:], equal[:], 0.0, ALU.mult, ALU.add).then_inc(step, 1)
            dve.wait_ge(sums_full, 1)
            dve.tensor_scalar(need, psum[:, 6, 0:1], -1.0, float(CAP), ALU.mult, ALU.add).then_inc(step, 1)
            dve.wait_ge(sums_full, 2)
            dve.tensor_copy(off_equal, psum[:, 7, 0:1]).then_inc(step, 1)
            dve.wait_ge(step, 5)
            dve.tensor_scalar(take[:], rank[:], off_equal, need, ALU.add, ALU.is_le).then_inc(step, 1)
            dve.wait_ge(step, 6)
            dve.tensor_tensor(lo[:], take[:], equal[:], ALU.mult).then_inc(keep_ready, 1)
            dve.wait_ge(keep_ready, BITS + 1)
            dve.tensor_tensor(take[:], lo[:], above[:], ALU.add).then_inc(keep_ready, 1)
            dve.wait_ge(keep_ready, BITS + 2)
            dve.tensor_tensor_scan(rank[:], ones[:], take[:], 0.0, ALU.mult, ALU.add).then_inc(step, 1)
            dve.wait_ge(sums_full, 3)
            dve.tensor_copy(off_take, psum[:, 5, 0:1]).then_inc(step, 1)
            dve.wait_ge(step, 8)
            dve.scalar_tensor_tensor(out=above[:], in0=rank[:], scalar=off_take, in1=take[:],
                                     op0=ALU.add, op1=ALU.mult).then_inc(step, 1)
            dve.wait_ge(step, 9)
            dve.tensor_scalar(equal[:], above[:], -1.0 - T // 2, 1.0 / T, ALU.add, ALU.mult).then_inc(step, 1)
            dve.wait_ge(step, 10)
            dve.tensor_scalar(hi[:], equal[:], ROUND, -ROUND, ALU.add, ALU.add).then_inc(step, 1)
            dve.wait_ge(step, 11)
            dve.scalar_tensor_tensor(out=lo[:], in0=hi[:], scalar=-float(T), in1=above[:],
                                     op0=ALU.mult, op1=ALU.add).then_inc(step, 1)
            dve.wait_ge(consts_ready, 1)
            dve.wait_ge(turned_out, 9)
            with dve.Fori(0, NC) as c:
                j = c + LOOPS
                lo_c = loT[:, bass.ds(c, 1), :].rearrange("p c n -> p (c n)")
                hi_c = hiT[:, bass.ds(c, 1), :].rearrange("p c n -> p (c n)")
                dve.tensor_tensor(hit[:], hi_c.unsqueeze(2).to_broadcast([T, 128, NC]),
                                  iota_hi[:].unsqueeze(1).to_broadcast([T, 128, NC]), ALU.is_equal).then_inc(hit_ready, 1)
                dve.wait_ge(hot_used, c)
                for f in range(FC + 1):
                    dve.tensor_tensor(hot_lo[:, f * 32:(f + 1) * 32, :],
                                      lo_c[:, f * 32:(f + 1) * 32].unsqueeze(2).to_broadcast([T, 32, T]),
                                      iota_lo[:].unsqueeze(1).to_broadcast([T, 32, T]), ALU.is_equal)
                    if f < FC:
                        shared_mult(dve, j, (f,))
                dve.wait_ge(hit_ready, c * 2 + 1)
                dve.tensor_tensor(hot_hi[:, :, 0:NC], hit[:], tile0[:].unsqueeze(2).to_broadcast([T, 128, NC]), ALU.mult)
                dve.tensor_scalar(hot_hi[:, :, NC:2 * NC], hit[:], row[:, 0:1], None, ALU.mult).then_inc(hot_ready, 1)
                dve.wait_ge(hot_ready, c + 1)
                dve.tensor_scalar(tile0[:], tile0[:], 1.0, None, ALU.add).then_inc(hit_ready, 1)
                shared_rows(dve, j)
            dve.wait_ge(ids_full, 1)
            dve.tensor_copy(idp[:], LISTS).then_inc(idp_ready, 1)
            dve.wait_ge(idT_full, 1)
            dve.tensor_copy(idT[:], psum[0:T, 7, :].rearrange("p (g n) -> p g n", g=4)).then_inc(idT_ready, 1)
            dve.wait_ge(idT_ready, 1)
            for q in range(4):
                last = dve.scalar_tensor_tensor(
                    out=ids.rearrange("p (g q) t -> p g q t", q=4)[:, :, q, :], in0=idT[:, :, 32 * q:32 * q + NC],
                    scalar=float(T), in1=idT[:, :, 32 * q + NC:32 * q + 2 * NC], op0=ALU.mult, op1=ALU.add)
            last.then_inc(ids_ready, 1)
            dve.wait_ge(ids_ready, 1)


def phase_experts(nc, psum, inp, xg, y, ids):
    FC = F0 // 128
    ROWW = D + E0
    CUTS = ((0, W4), (W4, W4), (2 * W4, SEQ - 2 * W4))
    G2 = DC * len(CUTS)
    UP = FC * len(CUTS)
    NP = NC // 2
    with ExitStack() as ctx:
        sb, sem = names(ctx, nc)
        ident = sb("ex_ident", [128, 128])
        wg = sb("ex_wg", [DP, 2, DC, F0])
        wu = sb("ex_wu", [DP, 2, DC, F0])
        wd = sb("ex_wd", [128, 2, FC, D])
        pad = sb("ex_pad", [128, 16])
        idx = sb("ex_idx", [T, 2, NC], I32)
        to = sb("ex_to", [T, 2, NC], I32)
        xs = sb("ex_xs", [T, 2, NC, ROWW])
        score = sb("ex_score", [T, 2, NC])
        xT = sb("ex_xT", [DP, DC, CAP])
        silu = sb("ex_silu", [128, 2, W4])
        hT = sb("ex_hT", [128, FC, CAP])
        ys = sb("ex_ys", [T, 2, NC, D])
        ident_in = sem("ex_ident_in")
        weights_in = [sem("ex_weights_in0"), sem("ex_weights_in1")]
        idx_ready, to_ready = sem("ex_idx_ready"), sem("ex_to_ready")
        gathered = [sem("ex_gathered0"), sem("ex_gathered1")]
        score_ready = sem("ex_score_ready")
        xT_full, xT_ready = sem("ex_xT_full"), sem("ex_xT_ready")
        g_full, u_full = sem("ex_g_full"), sem("ex_u_full")
        silu_ready, hT_ready = sem("ex_silu_ready"), sem("ex_hT_ready")
        d_full, ys_ready = sem("ex_d_full"), sem("ex_ys_ready")
        used = [sem("ex_used0"), sem("ex_used1")]
        added = sem("ex_added")
        GATHER = 16 * NC

        block = ctx.enter_context(nc.Block())

        @block.sync
        def _(sp):
            sp.dma_start(ident[:], inp["ident"]).then_inc(ident_in, 16)
            with sp.Fori(0, E0 // 2) as i:
                for half in range(2):
                    e = i * 2 + half
                    sp.wait_ge(used[half], i)
                    for dst, src, n in ((wg, "e0_gT", DC), (wu, "e0_uT", DC), (wd, "e0_dT", FC)):
                        sp.dma_start(dst[:, half], inp[src][bass.ds(e, 1)].rearrange("a (c p) n -> p (a c) n", c=n)) \
                            .then_inc(weights_in[half], 16)

        @block.gpsimd
        def _(pool):
            def carry(k):
                pool.tensor_tensor(pad[:, k:k + 1], ident[:, 0:1], ident[:, 0:1], ALU.add)

            pool.wait_ge(ident_in, 16)

            def gather(e, half, turned=True):
                if turned:
                    carry(14 + half)
                pool.tensor_copy(idx[:, half, :], ids[:, bass.ds(e, 1), :].rearrange("p a t -> p (a t)")) \
                    .then_inc(idx_ready, 1)
                pool.wait_ge(idx_ready, e + 1)
                if turned:
                    pool.wait_ge(xT_full, (e - 1) * G2)
                    pool.wait_ge(score_ready, e - 1)
                carry(half * 6)
                for t in range(NC):
                    pool.indirect_dma_start(xs[:, half, t, :], None, xg,
                                            bass.IndirectOffsetOnAxis(ap=idx[:, half, t:t + 1], axis=0)) \
                        .then_inc(gathered[half], 16)

            def scatter(e, half):
                pool.wait_ge(added, e * GATHER)
                carry(12 + half)
                pool.tensor_copy(to[:, half, :], ids[:, bass.ds(e, 1), :].rearrange("p a t -> p (a t)")) \
                    .then_inc(to_ready, 1)
                pool.wait_ge(to_ready, e + 1)
                for t in range(NC):
                    if t % 2 == 0:
                        pool.wait_ge(ys_ready, e * NP + (t // 2 + 1))
                        carry(half * 6 + 1 + t // 2)
                    pool.indirect_dma_start(y, bass.IndirectOffsetOnAxis(ap=to[:, half, t:t + 1], axis=0),
                                            ys[:, half, t, :], None, compute_op=ALU.add).then_inc(added, 16)

            gather(0, 0, False)
            with pool.Fori(0, E0 // 2 - 1) as i:
                for half in range(2):
                    e = i * 2 + half
                    pool.wait_ge(gathered[1 - half], i * GATHER + GATHER * half)
                    gather(e + 1, 1 - half)
                    scatter(e, half)
            pool.wait_ge(gathered[1], (E0 // 2 - 1) * GATHER)
            gather(E0 - 1, 1)
            scatter(E0 - 2, 0)
            scatter(E0 - 1, 1)
            pool.wait_ge(added, E0 * GATHER)

        def turn(pe, e, half):
            for n, (at, width) in enumerate(CUTS):
                for m in range(DC):
                    j = n * DC + m
                    if j < 2:
                        pe.wait_ge(xT_ready, e * G2)
                    else:
                        pe.wait_ge(xT_ready, e * G2 + (j - 1))
                    for t in range(at // T, (at + width) // T):
                        last = pe.transpose(psum[0:DP, 6 + m, t * T - at:(t + 1) * T - at],
                                            xs[:, half, t, m * DP:(m + 1) * DP], ident[0:T, 0:T])
                    last.then_inc(xT_full, 1)

        @block.tensor
        def _(pe):
            def up(e, half):
                for n, (at, width) in enumerate(CUTS):
                    pe.wait_ge(xT_ready, e * G2 + DC * (n + 1))
                    for f in range(FC):
                        j = n * FC + f
                        pe.wait_ge(hT_ready, e * UP + max(j - 1, 0))
                        for w, k0, full in ((wg, 0, g_full), (wu, 1, u_full)):
                            for k in range(DC):
                                mm = pe.matmul(psum[:, 2 * (j % 2) + k0, 0:width], w[:, half, k, f * 128:(f + 1) * 128],
                                               xT[:, k, at:at + width], start=(k == 0), stop=(k == 1))
                            mm.then_inc(full, 1)

            def down(e, half):
                for p in range(NP):
                    pe.wait_ge(hT_ready, e * UP + FC * ((2 * p + 1) // 4 + 1))
                    pe.wait_ge(ys_ready, e * NP + max(p - 1, 0))
                    for t in (2 * p, 2 * p + 1):
                        for f in range(FC):
                            mm = pe.matmul(psum[0:T, 4 + p % 2, (t % 2) * D:(t % 2 + 1) * D],
                                           hT[:, f, t * T:(t + 1) * T], wd[:, half, f, :],
                                           start=(f == 0), stop=(f == FC - 1))
                    mm.then_inc(d_full if p < NP - 1 else used[half], 1)

            pe.wait_ge(ident_in, 16)
            pe.wait_ge(gathered[0], GATHER)
            turn(pe, 0, 0)
            with pe.Fori(0, E0 // 2 - 1) as i:
                for half in range(2):
                    e = i * 2 + half
                    pe.wait_ge(weights_in[half], i * 48 + 48)
                    up(e, half)
                    pe.wait_ge(gathered[1 - half], i * GATHER + GATHER * (1 + half))
                    turn(pe, e + 1, 1 - half)
                    down(e, half)
            pe.wait_ge(weights_in[0], 48 * E0 // 2)
            up(E0 - 2, 0)
            pe.wait_ge(gathered[1], GATHER * E0 // 2)
            turn(pe, E0 - 1, 1)
            down(E0 - 2, 0)
            pe.wait_ge(weights_in[1], 48 * E0 // 2)
            up(E0 - 1, 1)
            down(E0 - 1, 1)

        @block.scalar
        def _(act):
            with act.Fori(0, E0) as e:
                for n, (at, width) in enumerate(CUTS):
                    for f in range(FC):
                        j = n * FC + f
                        act.wait_ge(g_full, e * UP + (j + 1))
                        act.wait_ge(hT_ready, e * UP + max(j - 1, 0))
                        act.activation(silu[:, j % 2, 0:width], psum[:, 2 * (j % 2), 0:width], ACT.Silu) \
                            .then_inc(silu_ready, 1)

        @block.vector
        def _(dve):
            def take_rows(e, half, n_gathered):
                dve.wait_ge(gathered[half], n_gathered)
                dve.tensor_copy(score[:, half, :], xs[:, half, :, bass.ds(e + D, 1)].rearrange("p t a -> p (t a)")) \
                    .then_inc(score_ready, 1)
                for n, (at, width) in enumerate(CUTS):
                    for m in range(DC):
                        dve.wait_ge(xT_full, e * G2 + (n * DC + m + 1))
                        dve.tensor_copy(xT[:, m, at:at + width], psum[0:DP, 6 + m, 0:width]).then_inc(xT_ready, 1)

            def hidden(e, half, n_used):
                for n, (at, width) in enumerate(CUTS):
                    for f in range(FC):
                        j = n * FC + f
                        dve.wait_ge(silu_ready, e * UP + (j + 1))
                        dve.wait_ge(u_full, e * UP + (j + 1))
                        if j == 0:
                            dve.wait_ge(used[1 - half], n_used)
                        dve.tensor_tensor(hT[:, f, at:at + width], silu[:, j % 2, 0:width],
                                          psum[:, 2 * (j % 2) + 1, 0:width], ALU.mult).then_inc(hT_ready, 1)

            def results(e, half, n_used):
                dve.wait_ge(score_ready, e + 1)
                for p in range(NP):
                    if p < NP - 1:
                        dve.wait_ge(d_full, e * (NP - 1) + (p + 1))
                    else:
                        dve.wait_ge(used[half], n_used)
                    dve.tensor_tensor(ys[:, half, 2 * p:2 * p + 2, :],
                                      psum[0:T, 4 + p % 2, 0:2 * D].rearrange("p (b d) -> p b d", b=2),
                                      score[:, half, 2 * p:2 * p + 2].unsqueeze(2).to_broadcast([T, 2, D]),
                                      ALU.mult).then_inc(ys_ready, 1)

            take_rows(0, 0, GATHER)
            with dve.Fori(0, E0 // 2 - 1) as i:
                for half in range(2):
                    e = i * 2 + half
                    hidden(e, half, i + half)
                    take_rows(e + 1, 1 - half, i * GATHER + GATHER * (1 + half))
                    results(e, half, i + 1)
            hidden(E0 - 2, 0, E0 // 2 - 1)
            take_rows(E0 - 1, 1, GATHER * E0 // 2)
            results(E0 - 2, 0, E0 // 2)
            hidden(E0 - 1, 1, E0 // 2)
            results(E0 - 1, 1, E0 // 2)


KT = 8
REST = SEQ - KT * 128
TILES = [(t, 128 * t, 128) for t in range(KT)] + [(KT, KT * 128, REST)]
HV = 32
QUADS = HEADS // 4


def image(dram, b):
    return dram.rearrange("(b n) d -> b n d", b=B)[bass.ds(b, 1)].rearrange("b n d -> (b n) d")


def layernorm_tiles(dve, c, rows, out, buf, sems, ready, tiles=TILES):
    stats, mv, std, rstd, pad = buf
    stats_ready, moments_ready, std_ready, rstd_ready = sems
    for t, _, n in tiles:
        last = dve.bn_stats(stats[0:n, t, :], rows[0:n, t, :])
    last.then_inc(stats_ready, 1)
    dve.wait_ge(stats_ready, c + 1)
    dve.memset(pad[:], 0.0)
    for t, _, n in tiles:
        last = dve.bn_aggr(mv[0:n, t, :], stats[0:n, t, :])
    last.then_inc(moments_ready, 1)
    dve.wait_ge(std_ready, c + 1)
    dve.reciprocal(rstd[:], std[:]).then_inc(rstd_ready, 1)
    dve.wait_ge(rstd_ready, c + 1)
    for t, _, n in tiles:
        dve.tensor_scalar(out[0:n, t, :], rows[0:n, t, :], mv[0:n, t, 0:1], rstd[0:n, t:t + 1],
                          ALU.subtract, ALU.mult).then_inc(ready, 1)


def phase_heads(nc, psum, inp, y, qk_parts, v_rows):
    NQ = 2 * D
    QC = NQ // DP
    CUTS = ((0, 512), (512, 512), (1024, REST))
    NB_X, NB_R = DC * 3, QC * 3
    with ExitStack() as ctx:
        sb, sem = names(ctx, nc)
        w = sb("hd_w", [DP, DC, NQ])
        ident = sb("hd_ident", [128, 128])
        cos = sb("hd_cos", [128, KT + 1, NQ])
        sin = sb("hd_sin", [128, KT + 1, NQ])
        gain = sb("hd_gain", [128, DH])
        shift = sb("hd_shift", [128, DH])
        eps = sb("hd_eps", [128, 1])
        rows = sb("hd_rows", [128, KT + 1, D])
        xn = sb("hd_xn", [128, KT + 1, D])
        xnT = sb("hd_xnT", [DP, DC, SEQ])
        part_c = sb("hd_part_c", [128, 2, NQ])
        part_s = sb("hd_part_s", [128, 2, NQ])
        rot = sb("hd_rot", [128, KT + 1, NQ])
        parts = sb("hd_parts", [DP, 3, QC, SEQ], BF16)
        left = sb("hd_left", [DP, 3, 512])
        NH = (KT + 1) * HEADS
        mean = sb("hd_mean", [128, NH])
        cen = sb("hd_cen", [128, NH, DH])
        square = sb("hd_square", [128, NH, DH])
        var = sb("hd_var", [128, NH])
        vstd = sb("hd_vstd", [128, NH])
        vrstd = sb("hd_vrstd", [128, NH])
        v_out = sb("hd_v_out", [128, NH, HV])
        stats = sb("hd_stats", [128, KT + 1, 6])
        mv = sb("hd_mv", [128, KT + 1, 2])
        std = sb("hd_std", [128, KT + 1])
        rstd = sb("hd_rstd", [128, KT + 1])
        pad = sb("hd_pad", [128, 1])

        consts_in, set_up = sem("hd_consts_in"), sem("hd_set_up")
        rows_in = sem("hd_rows_in")
        ln = [sem(f"hd_{n}") for n in ("stats_ready", "moments_ready", "std_ready", "rstd_ready")]
        xn_ready = sem("hd_xn_ready")
        xT_full, xT_ready = sem("hd_xT_full"), sem("hd_xT_ready")
        qk_full, turned = sem("hd_qk_full"), sem("hd_turned")
        rot_ready = sem("hd_rot_ready")
        rT_full = sem("hd_rT_full")
        p1_ready, left_ready = sem("hd_p1_ready"), sem("hd_left_ready")
        p2_ready, p3_ready = sem("hd_p2_ready"), sem("hd_p3_ready")
        v_mean, cen_ready = sem("hd_v_mean"), sem("hd_cen_ready")
        v_step, v_ready = sem("hd_v_step"), sem("hd_v_ready")
        sq_ready, vstd_ready = sem("hd_sq_ready"), sem("hd_vstd_ready")
        parts_out, v_stored = sem("hd_parts_out"), sem("hd_v_stored")
        NT = KT + 1

        kv = rot[:, :, D:NQ].rearrange("p t (h d) -> p t h d", h=HEADS)
        by_tile = lambda a: a.rearrange("p (t h) d -> p t h d", t=NT)
        wide = lambda a: a.rearrange("p (t h) -> p t h", t=NT).unsqueeze(3).to_broadcast([128, NT, HEADS, DH])

        block = ctx.enter_context(nc.Block())

        @block.sync
        def _(sp):
            for dst, src in ((w[:, :, 0:D], inp["L1_attn_Wq"].rearrange("(c p) n -> p c n", c=DC)),
                             (w[:, :, D:NQ], inp["L1_attn_Wkv"].rearrange("(c p) n -> p c n", c=DC)),
                             (ident[:], inp["ident"]),
                             (cos[:], inp["rope_cos"].rearrange("(t p) n -> p t n", p=128)),
                             (sin[:], inp["rope_sin"].rearrange("(t p) n -> p t n", p=128)),
                             (gain[:], spread(inp["L1_attn_ln_g"], 128)),
                             (shift[:], spread(inp["L1_attn_ln_b"], 128))):
                sp.dma_start(dst, src).then_inc(consts_in, 16)
            sp.wait_ge(set_up, 7)

            def load(b):
                src = image(y, b)
                sp.dma_start(rows[:, 0:KT, :], src[0:KT * 128].rearrange("(t p) d -> p t d", p=128)).then_inc(rows_in, 16)
                sp.dma_start(rows[0:REST, KT, :], src[KT * 128:SEQ]).then_inc(rows_in, 16)

            def store(b):
                sp.wait_ge(p3_ready, b * NB_R + NB_R)
                sp.dma_start(qk_parts[bass.ds(b, 1)].rearrange("b s c p n -> p (b s) c n"), parts[:]).then_inc(parts_out, 16)
                sp.wait_ge(v_ready, b * 2 + 2)
                dst = image(v_rows, b)
                sp.dma_start(dst[0:KT * 128].rearrange("(t p) n -> p t n", p=128),
                             v_out[:, 0:KT * HEADS, :].rearrange("p (t h) n -> p t (h n)", t=KT)).then_inc(v_stored, 16)
                sp.dma_start(dst[KT * 128:SEQ], v_out[0:REST, KT * HEADS:, :].rearrange("p h n -> p (h n)")) \
                    .then_inc(v_stored, 16)

            load(0)
            with sp.Fori(0, B - 1) as b:
                sp.wait_ge(xn_ready, b * NT + NT)
                load(b + 1)
                store(b)
            store(B - 1)
            sp.wait_ge(parts_out, 16 * B)
            sp.wait_ge(v_stored, 32 * B)

        @block.gpsimd
        def _(pool):
            pool.memset(eps[:], EPS).then_inc(set_up, 1)
            pool.memset(v_out[:, :, DH:DH + 1], 1.0).then_inc(set_up, 1)
            pool.memset(v_out[:, :, DH + 1:HV], 0.0).then_inc(set_up, 1)
            pool.memset(rows[:, KT, :], 0.0).then_inc(set_up, 1)
            pool.memset(rot[:, KT, :], 0.0).then_inc(set_up, 1)
            pool.memset(mv[:, KT, :], 1.0).then_inc(set_up, 1)
            pool.memset(xn[:, KT, :], 0.0).then_inc(set_up, 1)
            pool.wait_ge(consts_in, 16 * 7)
            pool.wait_ge(set_up, 7)
            with pool.Fori(0, B) as b:
                pool.wait_ge(rT_full, b * NB_R)
                pool.wait_ge(cen_ready, b)
                for t, _, n in TILES:
                    pool.wait_ge(turned, b * NT + (t + 1))
                    pool.tensor_tensor(rot[0:n, t, :], part_c[0:n, t % 2, :], part_s[0:n, t % 2, :],
                                       ALU.add).then_inc(rot_ready, 1)
                pool.wait_ge(parts_out, b * 16)
                for q in range(QC):
                    for s, (at, n) in enumerate(CUTS):
                        j = q * 3 + s
                        pool.wait_ge(p2_ready, b * NB_R + (j + 1))
                        pool.tensor_tensor(parts[:, 2, q, at:at + n], left[:, j % 3, 0:n],
                                           parts[:, 1, q, at:at + n], ALU.subtract).then_inc(p3_ready, 1)

        @block.tensor
        def _(pe):
            pe.wait_ge(consts_in, 16 * 7)
            with pe.Fori(0, B) as b:
                pe.wait_ge(p1_ready, b * NB_R)
                pe.wait_ge(left_ready, b * NB_R)
                for m in range(DC):
                    for s, (at, n) in enumerate(CUTS):
                        tiles = [x for x in TILES if at <= x[1] < at + n]
                        pe.wait_ge(xn_ready, b * NT + (tiles[-1][0] + 1))
                        for t, a, r in tiles:
                            last = pe.transpose(psum[0:DP, m * 3 + s, a - at:a - at + 128], xn[:, t, m * DP:(m + 1) * DP],
                                                ident[:])
                        last.then_inc(xT_full, 1)
                pe.wait_ge(xT_ready, b * NB_X + NB_X)
                for t, a, r in TILES:
                    if t >= 2:
                        pe.wait_ge(turned, b * NT + (t - 1))
                    for k in range(DC):
                        last = pe.matmul(psum[0:r, 6 + t % 2, 0:NQ], xnT[:, k, a:a + r], w[:, k, :],
                                         start=(k == 0), stop=(k == 1))
                    last.then_inc(qk_full, 1)
                for q in range(QC):
                    for s, (at, n) in enumerate(CUTS):
                        j = q * 3 + s
                        if j >= 6:
                            pe.wait_ge(left_ready, b * NB_R + (j - 5))
                        tiles = [x for x in TILES if at <= x[1] < at + n]
                        pe.wait_ge(rot_ready, b * NT + (tiles[-1][0] + 1))
                        for t, a, r in tiles:
                            last = pe.transpose(psum[0:DP, j % 6, a - at:a - at + 128], rot[:, t, q * DP:(q + 1) * DP],
                                                ident[:])
                        last.then_inc(rT_full, 1)

        @block.scalar
        def _(act):
            act.wait_ge(set_up, 7)

            def second_part(b, j):
                q, (at, n) = j // 3, CUTS[j % 3]
                act.wait_ge(left_ready, b * NB_R + (j + 1))
                act.activation(parts[:, 1, q, at:at + n], left[:, j % 3, 0:n], ACT.Identity).then_inc(p2_ready, 1)

            def root(b):
                act.wait_ge(ln[1], b + 1)
                act.activation(std[:], mv[:, :, 1], ACT.Sqrt, bias=eps[:]).then_inc(ln[2], 1)

            def image_steps(b, following):
                act.wait_ge(qk_full, b * NT)
                for m in range(DC):
                    for s, (at, n) in enumerate(CUTS):
                        act.wait_ge(xT_full, b * NB_X + (m * 3 + s + 1))
                        act.activation(xnT[:, m, at:at + n], psum[0:DP, m * 3 + s, 0:n], ACT.Identity).then_inc(xT_ready, 1)
                if following:
                    root(b + 1)
                act.wait_ge(parts_out, b * 16)
                for q in range(QC):
                    for s, (at, n) in enumerate(CUTS):
                        j = q * 3 + s
                        act.wait_ge(rT_full, b * NB_R + (j + 1))
                        act.activation(parts[:, 0, q, at:at + n], psum[0:DP, j % 6, 0:n], ACT.Identity).then_inc(p1_ready, 1)
                        if j:
                            second_part(b, j - 1)
                second_part(b, NB_R - 1)
                act.wait_ge(cen_ready, b + 1)
                act.activation(square[:], cen[:], ACT.Square).then_inc(sq_ready, 1)
                act.wait_ge(v_step, b * 4 + 2)
                act.activation(vstd[:], var[:], ACT.Sqrt, scale=1.0 / DH, bias=eps[:]).then_inc(vstd_ready, 1)

            root(0)
            with act.Fori(0, B - 1) as b:
                image_steps(b, True)
            image_steps(B - 1, False)

        @block.vector
        def _(dve):
            dve.wait_ge(consts_in, 16 * 7)
            dve.wait_ge(set_up, 7)
            def normalize(b):
                dve.wait_ge(rows_in, b * 32 + 32)
                dve.wait_ge(xT_full, b * NB_X)
                layernorm_tiles(dve, b, rows, xn, (stats, mv, std, rstd, pad), ln, xn_ready)

            def image_steps(b, following):
                for t, _, n in TILES:
                    dve.wait_ge(qk_full, b * NT + (t + 1))
                    dve.wait_ge(rot_ready, b * NT + max(t - 1, 0))
                    qk = psum[0:n, 6 + t % 2, 0:NQ]
                    halves = qk.rearrange("p (h k d) -> p h k d", k=2, d=DH // 2)
                    out = part_s[0:n, t % 2, :].rearrange("p (h k d) -> p h k d", k=2, d=DH // 2)
                    s = sin[0:n, t, :].rearrange("p (h k d) -> p h k d", k=2, d=DH // 2)
                    dve.tensor_tensor(part_c[0:n, t % 2, :], qk, cos[0:n, t, :], ALU.mult)
                    dve.tensor_tensor(out[:, :, 0, :], halves[:, :, 1, :], s[:, :, 0, :], ALU.mult)
                    dve.tensor_tensor(out[:, :, 1, :], halves[:, :, 0, :], s[:, :, 1, :], ALU.mult).then_inc(turned, 1)
                dve.wait_ge(rot_ready, b * NT + NT)
                dve.tensor_reduce(mean[:].rearrange("p (t h) -> p t h", t=NT), kv, AX_X, ALU.add).then_inc(v_mean, 1)
                dve.wait_ge(v_mean, b + 1)
                dve.tensor_scalar(mean[:], mean[:], 1.0 / DH, None, ALU.mult).then_inc(v_step, 1)
                dve.wait_ge(v_step, b * 4 + 1)
                dve.wait_ge(v_ready, b * 2)
                dve.tensor_tensor(by_tile(cen[:]), kv, wide(mean[:]), ALU.subtract).then_inc(cen_ready, 1)
                if following:
                    normalize(b + 1)
                for q in range(QC):
                    for s, (at, n) in enumerate(CUTS):
                        j = q * 3 + s
                        dve.wait_ge(p1_ready, b * NB_R + (j + 1))
                        dve.wait_ge(p3_ready, b * NB_R + max(j - 2, 0))
                        dve.tensor_tensor(left[:, j % 3, 0:n], psum[0:DP, j % 6, 0:n], parts[:, 0, q, at:at + n],
                                          ALU.subtract).then_inc(left_ready, 1)
                dve.wait_ge(sq_ready, b + 1)
                dve.tensor_reduce(var[:], square[:], AX_X, ALU.add).then_inc(v_step, 1)
                dve.wait_ge(vstd_ready, b + 1)
                dve.reciprocal(vrstd[:], vstd[:]).then_inc(v_step, 1)
                dve.wait_ge(v_step, b * 4 + 3)
                dve.tensor_tensor(cen[:], cen[:], vrstd[:].unsqueeze(2).to_broadcast([128, NH, DH]), ALU.mult) \
                    .then_inc(v_step, 1)
                dve.wait_ge(v_step, b * 4 + 4)
                dve.wait_ge(v_stored, b * 32)
                g = gain[:].unsqueeze(1).to_broadcast([128, NH, DH])
                z = shift[:].unsqueeze(1).to_broadcast([128, NH, DH])
                dve.tensor_tensor(square[:], cen[:], g, ALU.mult).then_inc(v_ready, 1)
                dve.wait_ge(v_ready, b * 2 + 1)
                dve.tensor_tensor(v_out[:, :, 0:DH], square[:], z, ALU.add).then_inc(v_ready, 1)

            normalize(0)
            with dve.Fori(0, B - 1) as b:
                image_steps(b, True)
            image_steps(B - 1, False)


def phase_attend(nc, psum, inp, qk_parts, v_rows, o_parts):
    R6 = 6 * DH
    RM = R6 + 3
    QH = 4
    CT = 8
    ctx_rows = [128] * 7 + [CTX - 7 * 128]
    HALVES = ((0, 512), (512, CTX - 512))
    QUARTERS = ((0, 256), (256, 256), (512, 244), (756, CTX - 756))
    LATS = ((0, 512), (512, 512), (1024, REST))
    NM = CT * QH + 1
    with ExitStack() as ctx:
        sb, sem = names(ctx, nc)
        identb = sb("at_identb", [128, 128], BF16)
        ident = sb("at_ident", [128, 128])
        Q = [sb(f"at_q{u}", [RM, QH * 1024 + QH * LAT], BF16) for u in range(3)]
        K = [sb(f"at_k{u}", [RM, QH, SEQ], BF16) for u in range(3)]
        V = [sb(f"at_v{u}", [128, KT + 1, QH * HV]) for u in range(3)]
        P = sb("at_p", [128, 2 * QH, CTX])
        PL = sb("at_pl", [128, QH * 256])
        PR = sb("at_pr", [REST, QH * LAT])
        mx = sb("at_mx", [128, 2, CT * QH])
        mxl = sb("at_mxl", [128, 3])
        nm = sb("at_nm", [128, NM])
        rest = sb("at_rest", [128, NM])
        M3 = sb("at_m3", [128, 3, NM], BF16)
        MT = sb("at_mt", [3 * NM, 128], BF16)
        O = sb("at_o", [128, SEQ])

        ident_in, identb_ready, ones_set = sem("at_ident_in"), sem("at_identb_ready"), sem("at_ones_set")
        loaded = [sem(f"at_loaded{u}") for u in range(3)]
        mrows = [sem(f"at_mrows{u}") for u in range(3)]
        s_full, s_free = sem("at_s_full"), sem("at_s_free")
        m_step = sem("at_m_step")
        st_full, exp_ready = sem("at_st_full"), sem("at_exp_ready")
        pv_full, o_ready, o_stored = sem("at_pv_full"), sem("at_o_ready"), sem("at_o_stored")
        LOAD, MROW = 20 * 16, 3 * 16
        ST_N = CT * QH + 2
        NG = B * QUADS
        MSTEP = 5
        MID = CT * QH // 2

        def exp_job(e):
            return e if e < MID else e + 2

        def combo(ahead, e):
            return [("half", ahead, e // QH, e % QH, h) for h in range(2)]

        def schedule(ahead):
            steps = [[] for _ in range(CT * QH)]
            if ahead >= 1:
                for e in range(24):
                    steps[e] += combo(1, e + 2 * QH)
                steps[24] += [("lats", k) for k in range(3)]
                steps[26] += [("turn",)]
            if ahead >= 2:
                for n, e in enumerate((25, 26, 27, 27, 28, 29, 30, 31)):
                    steps[e] += combo(2, n)
            steps[20] += [("latents_out",)]
            return steps

        PRO = [combo(0, e) for e in range(CT * QH)] + [[("lats", k) for k in range(3)], [("turn",)]] \
            + [combo(1, e) for e in range(2 * QH)]
        flat = lambda steps: [job for step in steps for job in step]
        PRE, QJ = len(flat(PRO)), len(flat(schedule(2)))
        LAST = {NG - 2: 1, NG - 1: 0}

        def base_of(g):
            return PRE + g * QJ

        END = base_of(NG - 2) + len(flat(schedule(1)))

        feats = qk_parts.rearrange("b s c p n -> b s (c p) n")
        QP, KP = (0, 0, 0, 1, 1, 2), (0, 1, 2, 0, 1, 0)

        block = ctx.enter_context(nc.Block())

        @block.sync
        def _(sp):
            sp.dma_start(ident[:], inp["ident"]).then_inc(ident_in, 16)

            def load(b, u):
                f = feats[bass.ds(b, 1)].rearrange("b s f n -> (b s) f n")
                for g in range(6):
                    q = f[QP[g], u * QH * DH:(u + 1) * QH * DH, :].rearrange("(j d) n -> d j n", j=QH)
                    k = f[KP[g], D + u * QH * DH:D + (u + 1) * QH * DH, :].rearrange("(j d) n -> d j n", j=QH)
                    rows = slice(g * DH, (g + 1) * DH)
                    sp.dma_start(Q[u][rows, 0:QH * 1024].rearrange("p (j n) -> p j n", j=QH)[:, :, 0:CTX],
                                 q[:, :, 0:CTX]).then_inc(loaded[u], 16)
                    sp.dma_start(Q[u][rows, QH * 1024:].rearrange("p (j n) -> p j n", j=QH),
                                 q[:, :, CTX:SEQ]).then_inc(loaded[u], 16)
                    sp.dma_start(K[u][rows, :, :], k).then_inc(loaded[u], 16)
                src = image(v_rows, b)[:, u * QH * HV:(u + 1) * QH * HV]
                sp.dma_start(V[u][:, 0:KT, :], src[0:KT * 128].rearrange("(t p) n -> p t n", p=128)).then_inc(loaded[u], 16)
                sp.dma_start(V[u][0:REST, KT, :], src[KT * 128:SEQ]).then_inc(loaded[u], 16)

            def put_maxima(u, jobs):
                sp.wait_ge(s_free, jobs)
                for s in range(3):
                    sp.dma_start(Q[u][R6 + s:R6 + s + 1, :].rearrange("a (r c) -> a r c", c=128),
                                 MT[s * NM:(s + 1) * NM, :]).then_inc(mrows[u], 16)

            def after(steps, job):
                return flat(steps).index(job) + 1

            load(0, 0)
            load(0, 1)
            put_maxima(0, after(PRO, ("turn",)))
            with sp.Fori(0, B - 1) as b:
                for u in range(3):
                    g = b * 3 + u
                    sp.wait_ge(pv_full, g * CT)
                    load(b + (u + 2) // 3, (u + 2) % 3)
                    put_maxima((u + 1) % 3, g * QJ + (PRE + after(schedule(2), ("turn",))))
            for u in range(2):
                g = (B - 1) * 3 + u
                if u == 0:
                    sp.wait_ge(pv_full, g * CT)
                    load(B - 1, 2)
                put_maxima(u + 1, base_of(g) + after(schedule(2 - u), ("turn",)))

        @block.gpsimd
        def _(pool):
            for u in range(3):
                pool.memset(K[u][R6:RM, :, :], 1.0).then_inc(ones_set, 1)
            pool.wait_ge(ones_set, 3)
            pool.memset(mx[:], 0.0).then_inc(ones_set, 1)
            pool.wait_ge(ones_set, 4)
            pool.wait_ge(ident_in, 16)
            pool.tensor_copy(identb[:], ident[:]).then_inc(identb_ready, 1)

            def store(b, u, g, jobs):
                pool.wait_ge(o_ready, g + 1)
                pool.wait_ge(s_free, jobs)
                dst = o_parts[bass.ds(b, 1), u].rearrange("b p n -> (b p) n")
                pool.dma_start(dst, O[:]).then_inc(o_stored, 16)

            out_at = lambda ahead: flat(schedule(ahead)).index(("latents_out",)) + 1
            with pool.Fori(0, B - 1) as b:
                for u in range(3):
                    store(b, u, b * 3 + u, (b * 3 + u) * QJ + (PRE + out_at(2)))
            for u in range(3):
                g = (B - 1) * 3 + u
                store(B - 1, u, g, (END if g == NG - 1 else base_of(g)) + out_at(2 - u))
            pool.wait_ge(o_stored, 16 * NG)

        @block.tensor
        def _(pe):
            pe.wait_ge(identb_ready, 1)
            pe.wait_ge(ones_set, 4)

            def job(what, n, base, u, g):
                bank = 4 + n % 2
                pe.wait_ge(s_free, base + max(n - 1, 0))
                if what[0] == "half":
                    _, ahead, t, j, h = what
                    v = (u + ahead) % 3
                    at, w = HALVES[h]
                    mm = pe.matmul(psum[0:ctx_rows[t], bank, 0:w],
                                   Q[v][0:R6, j * 1024 + 128 * t:j * 1024 + 128 * t + ctx_rows[t]],
                                   K[v][0:R6, j, at:at + w], start=True, stop=True)
                elif what[0] == "lats":
                    v = (u + 1) % 3
                    at, w = LATS[what[1]]
                    for j in range(QH):
                        mm = pe.matmul(psum[32 * j:32 * j + LAT, bank, 0:w],
                                       Q[v][0:R6, QH * 1024 + j * LAT:QH * 1024 + (j + 1) * LAT],
                                       K[v][0:R6, j, at:at + w], start=True, stop=True)
                elif what[0] == "turn":
                    pe.wait_ge(m_step, g * MSTEP + 2 * MSTEP)
                    mm = pe.transpose(psum[:, bank, :].bitcast(BF16)[0:3 * NM, 0:128],
                                      M3[:].rearrange("p s n -> p (s n)"), identb[:])
                else:
                    pe.wait_ge(exp_ready, g * ST_N + (MID + 2))
                    for t in range(KT + 1):
                        for j in range(QH):
                            w = V[u][:, t, j * HV:(j + 1) * HV] if t < KT else V[u][0:REST, t, j * HV:(j + 1) * HV]
                            x = PL[:, j * 256 + t * LAT:j * 256 + (t + 1) * LAT] if t < KT else PR[:, j * LAT:(j + 1) * LAT]
                            mm = pe.matmul(psum[32 * j:32 * j + HV, bank, 0:LAT], w, x, start=(t == 0), stop=(t == KT))
                mm.then_inc(s_full, 1)

            def latents_scores(u, g):
                pe.wait_ge(exp_ready, g * ST_N + (MID - 1))
                for j in range(QH):
                    for t in range(KT):
                        at = j * 256 + t * LAT
                        mm = pe.matmul(psum[:, at // 512, at % 512:at % 512 + LAT], K[u][:, j, 128 * t:128 * t + 128],
                                       Q[u][:, QH * 1024 + j * LAT:QH * 1024 + (j + 1) * LAT], start=True, stop=True)
                mm.then_inc(st_full, 1)
                pe.wait_ge(exp_ready, g * ST_N + MID)
                for j in range(QH):
                    mm = pe.matmul(psum[0:REST, 2, j * LAT:(j + 1) * LAT], K[u][:, j, KT * 128:SEQ],
                                   Q[u][:, QH * 1024 + j * LAT:QH * 1024 + (j + 1) * LAT], start=True, stop=True)
                mm.then_inc(st_full, 1)

            def values(u, g, t, s):
                if s == 0:
                    pe.wait_ge(exp_ready, g * ST_N + (exp_job((t + 1) * QH - 1) + 1))
                    if t == 0:
                        pe.wait_ge(o_ready, g)
                n = ctx_rows[t]
                at, w = QUARTERS[s]
                for j in range(QH):
                    mm = pe.matmul(psum[32 * j:32 * j + HV, 6 + at // 512, at % 512:at % 512 + w],
                                   V[u][0:n, t, j * HV:(j + 1) * HV], P[0:n, (t % 2) * QH + j, at:at + w],
                                   start=(t == 0 and s % 2 == 0), stop=(t == CT - 1 and s % 2 == 1),
                                   skip_group_check=True)
                if s == 3:
                    mm.then_inc(pv_full, 1)

            def exp_step(b, u, g, base, ahead):
                n = 0
                pe.wait_ge(mrows[u], b * MROW + MROW)
                for e, jobs in enumerate(schedule(ahead)):
                    t, j = e // QH, e % QH
                    if e == MID:
                        latents_scores(u, g)
                    x = exp_job(e)
                    pe.wait_ge(exp_ready, g * ST_N + max(x - 1, 0))
                    for h, (at, w) in enumerate(HALVES):
                        mm = pe.matmul(psum[0:ctx_rows[t], 2 * (e % 2) + h, 0:w],
                                       K[u][:, j, 128 * t:128 * t + ctx_rows[t]], Q[u][:, j * 1024 + at:j * 1024 + at + w],
                                       start=True, stop=True)
                    mm.then_inc(st_full, 1)
                    for k, what in enumerate(jobs):
                        if k == 1 and t >= 1:
                            values(u, g, t - 1, j)
                        if what == ("half", 2, 0, 0, 0):
                            pe.wait_ge(loaded[(u + 2) % 3], (b + (u + 2) // 3) * LOAD + LOAD)
                        job(what, n, base, u, g)
                        n += 1
                    if t >= 1 and len(jobs) < 2:
                        values(u, g, t - 1, j)
                for s in range(4):
                    values(u, g, CT - 1, s)

            pe.wait_ge(loaded[0], LOAD)
            pe.wait_ge(loaded[1], LOAD)
            for n, what in enumerate(flat(PRO)):
                if what[0] == "half":
                    job(what, n, 0, 0, 0)
                else:
                    job(what, n, 0, -1, -1)
            with pe.Fori(0, B - 1) as b:
                for u in range(3):
                    exp_step(b, u, b * 3 + u, (b * 3 + u) * QJ + PRE, 2)
            for u in range(3):
                g = (B - 1) * 3 + u
                exp_step(B - 1, u, g, END if g == NG - 1 else base_of(g), 2 - u)

        @block.scalar
        def _(act):
            def latents_exps(g):
                act.wait_ge(st_full, g * ST_N + (MID + 1))
                act.wait_ge(o_ready, g)
                act.activation(PL[:], psum[:, 0:2, :].rearrange("p a n -> p (a n)"), ACT.Exp).then_inc(exp_ready, 1)
                act.wait_ge(st_full, g * ST_N + (MID + 2))
                act.activation(PR[:], psum[0:REST, 2, 0:QH * LAT], ACT.Exp).then_inc(exp_ready, 1)

            def quad(g):
                for e in range(CT * QH):
                    if e == MID:
                        latents_exps(g)
                    t = e // QH
                    n = ctx_rows[t]
                    act.wait_ge(st_full, g * ST_N + (exp_job(e) + 1))
                    act.wait_ge(pv_full, g * CT + max(t - 1, 0))
                    act.activation(P[0:n, e % (2 * QH), :],
                                   psum[0:n, 2 * (e % 2):2 * (e % 2) + 2, :].rearrange("p a n -> p (a n)")[:, 0:CTX],
                                   ACT.Exp).then_inc(exp_ready, 1)
                act.wait_ge(pv_full, g * CT + CT)
                act.wait_ge(o_stored, g * 16)
                act.activation(O[:, 0:CTX], psum[:, 6:8, :].rearrange("p a n -> p (a n)")[:, 0:CTX],
                               ACT.Identity).then_inc(o_ready, 1)
            with act.Fori(0, NG) as g:
                quad(g)

        @block.vector
        def _(dve):
            dve.wait_ge(ones_set, 4)

            def parts(q):
                dve.tensor_tensor(nm[:, 0:NM - 1], mx[:, 0, :], mx[:, 1, :], ALU.max)
                dve.tensor_reduce(nm[:, NM - 1:NM], mxl[:], AX_X, ALU.max).then_inc(m_step, 1)
                dve.wait_ge(m_step, q * MSTEP + 1)
                dve.tensor_scalar(M3[:, 0, :], nm[:], -1.0, None, ALU.mult).then_inc(m_step, 1)
                dve.wait_ge(m_step, q * MSTEP + 2)
                dve.scalar_tensor_tensor(out=rest[:], in0=nm[:], scalar=-1.0, in1=M3[:, 0, :],
                                         op0=ALU.mult, op1=ALU.subtract).then_inc(m_step, 1)
                dve.wait_ge(m_step, q * MSTEP + 3)
                dve.tensor_copy(M3[:, 1, :], rest[:]).then_inc(m_step, 1)
                dve.wait_ge(m_step, q * MSTEP + 4)
                dve.tensor_tensor(M3[:, 2, :], rest[:], M3[:, 1, :], ALU.subtract).then_inc(m_step, 1)

            def take(jobs, base, g):
                for n, what in enumerate(jobs):
                    bank = 4 + n % 2
                    dve.wait_ge(s_full, base + (n + 1))
                    if what[0] == "half":
                        _, _, t, j, h = what
                        dve.tensor_reduce(mx[0:ctx_rows[t], h, j * CT + t:j * CT + t + 1],
                                          psum[0:ctx_rows[t], bank, 0:HALVES[h][1]], AX_X, ALU.max).then_inc(s_free, 1)
                    elif what[0] == "lats":
                        k = what[1]
                        dve.tensor_reduce(mxl[:, k:k + 1], psum[:, bank, 0:LATS[k][1]], AX_X, ALU.max).then_inc(s_free, 1)
                        if k == 2:
                            dve.wait_ge(s_free, base + (n + 1))
                            parts(g + 1)
                    elif what[0] == "turn":
                        dve.tensor_copy(MT[:], psum[:, bank, :].bitcast(BF16)[0:3 * NM, 0:128]).then_inc(s_free, 1)
                    else:
                        dve.wait_ge(o_stored, g * 16)
                        dve.tensor_copy(O[:, CTX:SEQ], psum[:, bank, 0:LAT]).then_inc(s_free, 1)

            take(flat(PRO), 0, -1)
            with dve.Fori(0, NG - 2) as g:
                take(flat(schedule(2)), g * QJ + PRE, g)
            take(flat(schedule(1)), base_of(NG - 2), NG - 2)
            take(flat(schedule(0)), END, NG - 1)


WS = 512
GS = WS // 128
PAD = WS
NCH = 42
NSL = NCH * GS
assert NCH >= (2 * TOK + E1 * (WS - 1)) // WS and NCH % 2 == 0
TC = [(t, 128 * t, 128) for t in range(7)] + [(7, 896, CTX - 896), (8, CTX, LAT)]
NTC = len(TC)



def phase_project(nc, psum, inp, o_parts, recips, h2, h3, x3T, logits, xg):
    NT = len(TC)
    CUTS = ((0, 512), (512, CTX - 512), (CTX, LAT))
    JOBS = [TC[0:2], TC[2:4], TC[4:6], TC[6:8], TC[8:9]]
    NJ, NX = len(JOBS), DC * len(CUTS)
    LOAD = 16 * 8
    CONSTS = 16 * (2 * (4 + 1) + 2)
    with ExitStack() as ctx:
        sb, sem = names(ctx, nc)
        wo = sb("pr_wo", [128, 2, QUADS, D])
        bias = sb("pr_bias", [128, 2, D])
        ident = sb("pr_ident", [128, 128])
        router = sb("pr_router", [DP, DC, E1])
        eps = sb("pr_eps", [128, 1])
        op = sb("pr_op", [128, 2, QUADS, SEQ])
        recip = sb("pr_recip", [128, 2, QUADS, SEQ])
        sums = sb("pr_sums", [B * HEADS, SEQ])
        shares = sb("pr_shares", [B * HEADS, SEQ])
        on = sb("pr_on", [128, QUADS, SEQ])
        hin = sb("pr_hin", [128, 2, NT, D])
        hb = sb("pr_hb", [128, NT, D])
        hout = sb("pr_hout", [128, NT, D])
        xn = sb("pr_xn", [128, NT, D])
        xT = sb("pr_xT", [DP, DC, SEQ])
        stats = sb("pr_stats", [128, NT, 6])
        mv = sb("pr_mv", [128, NT, 2])
        std = sb("pr_std", [128, NT])
        rstd = sb("pr_rstd", [128, NT])
        pad = sb("pr_pad", [128, 1])

        zeroed, consts_in = sem("pr_zeroed"), sem("pr_consts_in")
        loaded = [sem("pr_loaded0"), sem("pr_loaded1")]
        sums_in, recip_ready, recip_stored = sem("pr_sums_in"), sem("pr_recip_ready"), sem("pr_recip_stored")
        scaled = [sem("pr_scaled0"), sem("pr_scaled1")]
        hb_ready = [sem("pr_hb_ready0"), sem("pr_hb_ready1")]
        o_full, h3_ready, h3_stored = sem("pr_o_full"), sem("pr_h3_ready"), sem("pr_h3_stored")
        ln = [sem(f"pr_{n}") for n in ("stats_ready", "moments_ready", "std_ready", "rstd_ready")]
        xn_ready, xT_full, xT_ready, xT_kept = sem("pr_xn_ready"), sem("pr_xT_full"), sem("pr_xT_ready"), sem("pr_xT_kept")
        l_full, l_ready = sem("pr_l_full"), sem("pr_l_ready")
        x3_stored = sem("pr_x3_stored")

        block = ctx.enter_context(nc.Block())

        def by_tiles(rows, buf):
            return ((rows[0:896].rearrange("(t p) d -> p t d", p=128), buf[:, 0:7, :]),
                    (rows[896:CTX], buf[0:CTX - 896, 7, :]), (rows[CTX:SEQ], buf[0:LAT, 8, :]))

        @block.sync
        def _(sp):
            sp.dma_start(sums[:], o_parts.rearrange("b q (j r) n -> (b q j) r n", r=32)[:, DH, :]).then_inc(sums_in, 16)
            sp.wait_ge(recip_ready, 1)
            sp.dma_start(recips.rearrange("b h n -> (b h) n"), shares[:]).then_inc(recip_stored, 16)
            sp.wait_ge(recip_stored, 16)
            sp.wait_ge(zeroed, 6)
            with sp.Fori(0, B // 2) as i:
                for half in range(2):
                    b = i * 2 + half
                    sp.wait_ge(scaled[half], i)
                    sp.wait_ge(hb_ready[half], i)
                    sp.dma_start(op[:, half], o_parts[bass.ds(b, 1)].rearrange("a q p n -> p (a q) n")) \
                        .then_inc(loaded[half], 16)
                    for j in range(4):
                        src = recips.rearrange("b (q j) n -> b j q n", j=4)[bass.ds(b, 1), j]
                        sp.dma_start(recip[32 * j:32 * j + 32, half], src.broadcast_to([32, QUADS, SEQ])) \
                            .then_inc(loaded[half], 16)
                    for src, dst in by_tiles(image(h2, b), hin[:, half]):
                        sp.dma_start(dst, src).then_inc(loaded[half], 16)

        @block.gpsimd
        def _(pool):
            for buf in (wo[:], hin[:], mv[:], xn[:], logits):
                pool.memset(buf, 0.0).then_inc(zeroed, 1)
            pool.memset(eps[:], EPS).then_inc(zeroed, 1)
            pool.wait_ge(consts_in, CONSTS)

            def add_bias(b, i, half):
                pool.wait_ge(loaded[half], i * LOAD + LOAD)
                pool.wait_ge(h3_ready, b * NJ)
                pool.tensor_tensor(hb[:, 0:8, :], hin[:, half, 0:8, :],
                                   bias[:, 0:1, :].to_broadcast([128, 8, D]), ALU.add)
                pool.tensor_tensor(hb[0:LAT, 8, :], hin[0:LAT, half, 8, :], bias[0:LAT, 1, :], ALU.add) \
                    .then_inc(hb_ready[half], 1)

            def keep(b):
                pool.wait_ge(xT_ready, b * NX + NX)
                pool.tensor_copy(x3T[:, :, bass.ds(b, 1), :].rearrange("p c a n -> p c (a n)"), xT[:]) \
                    .then_inc(xT_kept, 1)

            add_bias(0, 0, 0)
            with pool.Fori(0, B // 2 - 1) as i:
                add_bias(i * 2 + 1, i, 1)
                keep(i * 2)
                add_bias(i * 2 + 2, i + 1, 0)
                keep(i * 2 + 1)
            add_bias(B - 1, B // 2 - 1, 1)
            keep(B - 2)
            keep(B - 1)

        @block.tensor
        def _(pe):
            pe.wait_ge(consts_in, CONSTS)

            def project(b, i, half):
                pe.wait_ge(scaled[half], i + 1)
                pe.wait_ge(h3_ready, b * NJ)
                for k, tiles in enumerate(JOBS):
                    for t, at, n in tiles:
                        for q in range(QUADS):
                            mm = pe.matmul(psum[0:n, k, (t % 2) * D:(t % 2 + 1) * D], on[:, q, at:at + n],
                                           wo[:, int(t == 8), q, :], start=(q == 0), stop=(q == QUADS - 1))
                    mm.then_inc(o_full, 1)

            def turn(b):
                for m in range(DC):
                    for s, (at, w) in enumerate(CUTS):
                        k = m * len(CUTS) + s
                        pe.wait_ge(xT_ready, b * NX + max(k - 1, 0))
                        tiles = [x for x in TC if at <= x[1] < at + w]
                        pe.wait_ge(xn_ready, b * NT + (tiles[-1][0] + 1))
                        for t, a, n in tiles:
                            mm = pe.transpose(psum[0:DP, 5 + k % 2, a - at:a - at + 128],
                                              xn[:, t, m * DP:(m + 1) * DP], ident[:])
                        mm.then_inc(xT_full, 1)
                pe.wait_ge(xT_ready, b * NX + NX)
                pe.wait_ge(l_ready, b)
                for t, at, n in TC:
                    for k in range(DC):
                        mm = pe.matmul(psum[0:n, 7, t * E1:(t + 1) * E1], xT[:, k, at:at + n], router[:, k, :],
                                       start=(k == 0), stop=(k == 1))
                mm.then_inc(l_full, 1)

            project(0, 0, 0)
            with pe.Fori(0, B // 2 - 1) as i:
                project(i * 2 + 1, i, 1)
                turn(i * 2)
                project(i * 2 + 2, i + 1, 0)
                turn(i * 2 + 1)
            project(B - 1, B // 2 - 1, 1)
            turn(B - 2)
            turn(B - 1)

        @block.scalar
        def _(act):
            act.wait_ge(zeroed, 6)
            for n, name in enumerate(("ctx", "lat")):
                heads = inp[f"L1_attn_Wo_{name}"].rearrange("(q j d) n -> j d q n", j=4, d=DH)
                for j in range(4):
                    act.dma_start(wo[32 * j:32 * j + DH, n, :, :], heads[j]).then_inc(consts_in, 16)
                act.dma_start(bias[:, n, :], spread(inp[f"L1_attn_bo_{name}"], 128)).then_inc(consts_in, 16)
            for dst, src in ((ident[:], inp["ident"]), (router[:], inp["routerT"].rearrange("(c p) e -> p c e", c=DC))):
                act.dma_start(dst, src).then_inc(consts_in, 16)
            tiles_logits = logits.rearrange("p (t b) e -> p t b e", b=B)
            with act.Fori(0, B) as b:
                act.wait_ge(h3_ready, b * NJ + NJ)
                for dst, src in by_tiles(image(h3, b), hout):
                    act.dma_start(dst, src).then_inc(h3_stored, 16)
                act.wait_ge(ln[1], b + 1)
                act.activation(std[:], mv[:, :, 1], ACT.Sqrt, bias=eps[:]).then_inc(ln[2], 1)
                act.wait_ge(xn_ready, b * NT + NT)
                for dst, src in by_tiles(image(xg[PAD:PAD + TOK, 0:D], b), xn):
                    act.dma_start(dst, src).then_inc(x3_stored, 16)
                act.wait_ge(xT_kept, b)
                act.wait_ge(l_full, b)
                for m in range(DC):
                    for s, (at, w) in enumerate(CUTS):
                        k = m * len(CUTS) + s
                        act.wait_ge(xT_full, b * NX + (k + 1))
                        act.activation(xT[:, m, at:at + w], psum[0:DP, 5 + k % 2, 0:w], ACT.Identity).then_inc(xT_ready, 1)
                act.wait_ge(l_full, b + 1)
                for t0, t1, n in ((0, 7, 128), (7, 8, CTX - 896), (8, 9, LAT)):
                    last = act.activation(tiles_logits[0:n, t0:t1, bass.ds(b, 1), :].rearrange("p t a e -> p t (a e)"),
                                          psum[0:n, 7, t0 * E1:t1 * E1].rearrange("p (t e) -> p t e", e=E1), ACT.Identity)
                last.then_inc(l_ready, 1)
            act.wait_ge(h3_stored, 48 * B)
            act.wait_ge(x3_stored, 48 * B)

        @block.vector
        def _(dve):
            def scale(b, i, half):
                dve.wait_ge(loaded[half], i * LOAD + LOAD)
                dve.wait_ge(o_full, b * NJ)
                dve.tensor_tensor(on[:], op[:, half], recip[:, half], ALU.mult).then_inc(scaled[half], 1)

            def image_steps(b, i, half, following):
                dve.wait_ge(h3_stored, b * 48)
                dve.wait_ge(xn_ready, b * NT)
                dve.wait_ge(hb_ready[half], i + 1)
                for k, tiles in enumerate(JOBS):
                    dve.wait_ge(o_full, b * NJ + (k + 1))
                    for t, _, n in tiles:
                        last = dve.tensor_tensor(hout[0:n, t, :], psum[0:n, k, (t % 2) * D:(t % 2 + 1) * D],
                                                 hb[0:n, t, :], ALU.add)
                    last.then_inc(h3_ready, 1)
                if following:
                    scale(*following)
                dve.wait_ge(xT_full, b * NX)
                dve.wait_ge(x3_stored, b * 48)
                dve.wait_ge(h3_ready, b * NJ + NJ)
                layernorm_tiles(dve, b, hout, xn, (stats, mv, std, rstd, pad), ln, xn_ready, TC)

            dve.wait_ge(sums_in, 16)
            dve.reciprocal(shares[:], sums[:]).then_inc(recip_ready, 1)
            dve.wait_ge(zeroed, 6)
            dve.wait_ge(consts_in, CONSTS)
            scale(0, 0, 0)
            with dve.Fori(0, B // 2 - 1) as i:
                image_steps(i * 2, i, 0, (i * 2 + 1, i, 1))
                image_steps(i * 2 + 1, i, 1, (i * 2 + 2, i + 1, 0))
            image_steps(B - 2, B // 2 - 1, 0, (B - 1, B // 2 - 1, 1))
            image_steps(B - 1, B // 2 - 1, 1, None)


def phase_dispatch(nc, psum, inp, h3, x3T, logits, y, xg, ids, chunk_expert, chunk_hot):
    N = NTC * B
    NP = B * E1
    NK = 2 * NTC
    FC = F1 // 128
    CUTS = ((0, W4), (W4, W4), (2 * W4, SEQ - 2 * W4))
    UP = FC * len(CUTS)
    NB = NC // 2
    ROUND = 1.5 * 2.0 ** 23
    with ExitStack() as ctx:
        sb, sem = names(ctx, nc)
        ident = sb("di_ident", [128, 128])
        ebias = sb("di_ebias", [128, E1])
        order = sb("di_order", [128, E1])
        before = sb("di_before", [NP, NP])
        same = sb("di_same", [NP, NP])
        lower = sb("di_lower", [NP, NP])
        firsts = sb("di_firsts", [NP, 128])
        chunks = sb("di_chunks", [NP, NCH])
        iotas32 = sb("di_iotas32", [128, 128 + NSL])
        codes32 = sb("di_codes32", [128, 2, B * NK])
        padrow = sb("di_padrow", [128, NSL])
        iota_lo = sb("di_iota_lo", [128, 128], BF16)
        iota_hi = sb("di_iota_hi", [128, NSL], BF16)
        codes = sb("di_codes", [128, 2, B, NK], BF16)
        expd = sb("di_expd", [128, N, E1])
        score = sb("di_score", [128, N, E1])
        pick = sb("di_pick", [128, N, E1])
        tie = sb("di_tie", [128, N, E1])
        picked = [sb(f"di_picked{k}", [128, N, E1]) for k in range(2)]
        best = sb("di_best", [128, N])
        mask = sb("di_mask", [NP, SEQ])
        ones = sb("di_ones", [NP, SEQ])
        rank = sb("di_rank", [NP, SEQ])
        small = sb("di_small", [NP, 8])
        reached = sb("di_reached", [NP, NCH])
        slot = sb("di_slot", [128, N, E1])
        sel = sb("di_sel", [128, B, 2, NTC])
        hi32 = sb("di_hi32", [128, B, NK])
        hi = sb("di_hi", [128, B, NK], BF16)
        lo = sb("di_lo", [128, B, NK], BF16)
        expert = sb("di_expert", [128, NCH])
        hot_lo = sb("di_hot_lo", [128, NK, 128], BF16)
        hit = sb("di_hit", [128, NK, NSL], BF16)
        hot_hi = sb("di_hot_hi", [128, NK, 2 * NSL], BF16)
        low_part = sb("di_low_part", [128, NSL])
        rows = sb("di_rows", [128, NSL])
        no_token = sb("di_no_token", [128, NSL])
        zero = sb("di_zero", [128, GS, D + E1])
        zerob = sb("di_zerob", [128, 2 * NSL], BF16)
        wg = sb("di_wg", [DP, DC, F1])
        wu = sb("di_wu", [DP, DC, F1])
        wd = sb("di_wd", [128, FC, D])
        silu = sb("di_silu", [128, 2, W4])
        hT = sb("di_hT", [128, FC, SEQ])
        h_in = sb("di_h_in", [T, NC, D])
        y_out = sb("di_y_out", [T, NC, D])

        zeroed, consts_in, tables = sem("di_zeroed"), sem("di_consts_in"), sem("di_tables")
        step = sem("di_step")
        exp_in, exp_ready = sem("di_exp_in"), sem("di_exp_ready")
        shares_ready, picks_ready, ranked = sem("di_shares_ready"), sem("di_picks_ready"), sem("di_ranked")
        chunks_ready, reached_ready, slots_ready = sem("di_chunks_ready"), sem("di_reached_ready"), sem("di_slots_ready")
        lists_ready = sem("di_lists_ready")
        shares_out, pads_out = sem("di_shares_out"), sem("di_pads_out")
        picks_turned, slots_turned, sums = sem("di_picks_turned"), sem("di_slots_turned"), sem("di_sums")
        hit_ready, hot_ready, hot_used = sem("di_hit_ready"), sem("di_hot_ready"), sem("di_hot_used")
        lists_full = sem("di_lists_full")
        g_full, u_full = sem("di_g_full"), sem("di_u_full")
        silu_ready, hT_ready = sem("di_silu_ready"), sem("di_hT_ready")
        d_full, y_ready = sem("di_d_full"), sem("di_y_ready")
        h_loaded, y_stored = sem("di_h_loaded"), sem("di_y_stored")
        CONSTS = 16 * 14

        h_img = h3.rearrange("(b n p) d -> b p n d", b=B, p=T)
        y_img = y[PAD:PAD + TOK].rearrange("(b n p) d -> b p n d", b=B, p=T)
        LISTS = psum[:, 6, 0:2 * NSL]

        block = ctx.enter_context(nc.Block())

        @block.sync
        def _(sp):
            for dst, src in ((ident[:], inp["ident"]), (ebias[:], spread(inp["L1_ffn_expert_bias"], 128)),
                             (order[:], inp["mix_order"]), (before[:], inp["di_before"]), (same[:], inp["di_same"]),
                             (lower[:], inp["di_lower"]), (firsts[:], inp["di_firsts"]), (chunks[:], inp["di_chunks"]),
                             (iotas32[:], inp["di_iotas"]), (codes32[:], inp["di_codes"]), (padrow[:], inp["di_padrow"]),
                             (wg[:], inp["s1_gT"].rearrange("(c p) f -> p c f", c=DC)),
                             (wu[:], inp["s1_uT"].rearrange("(c p) f -> p c f", c=DC)),
                             (wd[:], inp["s1_dT"].rearrange("(c p) d -> p c d", c=FC))):
                sp.dma_start(dst, src).then_inc(consts_in, 16)
            with sp.Fori(0, B) as b:
                sp.wait_ge(y_ready, b * NB)
                sp.dma_start(h_in[:], h_img[bass.ds(b, 1)].rearrange("b p n d -> p (b n) d")).then_inc(h_loaded, 16)
                sp.wait_ge(y_ready, b * NB + NB)
                sp.dma_start(y_img[bass.ds(b, 1)].rearrange("b p n d -> p (b n) d"), y_out[:]).then_inc(y_stored, 16)
            sp.wait_ge(y_stored, 16 * B)

        @block.gpsimd
        def _(pool):
            pool.memset(zero[:], 0.0).then_inc(zeroed, 1)
            pool.memset(zerob[:], 0.0).then_inc(zeroed, 1)
            pool.memset(ones[:], 1.0).then_inc(zeroed, 1)
            pool.memset(slot[:], -1e6).then_inc(zeroed, 1)
            pool.wait_ge(zeroed, 4)
            pool.dma_start(xg[0:PAD].rearrange("(t p) d -> p t d", p=128), zero[:]).then_inc(pads_out, 16)
            pool.dma_start(y[0:PAD].rearrange("(t p) d -> p t d", p=128), zero[:, :, 0:D]).then_inc(pads_out, 16)
            pool.wait_ge(shares_ready, 1)
            share_rows = xg[PAD:PAD + TOK, D:].rearrange("(b n) e -> n b e", b=B)
            shares = expd[:].rearrange("p (t b) e -> p t b e", b=B)
            for t, at, n in TC:
                pool.dma_start(share_rows[at:at + n], shares[0:n, t, :, :]).then_inc(shares_out, 16)
            pool.wait_ge(shares_out, 16 * NTC)
            pool.wait_ge(pads_out, 32)

        def shared_up(pe, b):
            for s, (at, w) in enumerate(CUTS):
                for f in range(FC):
                    j = s * FC + f
                    pe.wait_ge(hT_ready, b * UP + max(j - 1, 0))
                    for k0, (wt, full) in enumerate(((wg, g_full), (wu, u_full))):
                        for k in range(DC):
                            mm = pe.matmul(psum[:, 2 * (j % 2) + k0, 0:w], wt[:, k, f * 128:(f + 1) * 128],
                                           x3T[:, k, bass.ds(b, 1), at:at + w].rearrange("p a n -> p (a n)"),
                                           start=(k == 0), stop=(k == 1))
                        mm.then_inc(full, 1)

        def shared_down(pe, b):
            for p in range(NB):
                pe.wait_ge(hT_ready, b * UP + FC * ((2 * p + 1) // 4 + 1))
                pe.wait_ge(y_ready, b * NB + max(p - 1, 0))
                for t in (2 * p, 2 * p + 1):
                    for f in range(FC):
                        mm = pe.matmul(psum[0:T, 4 + p % 2, (t % 2) * D:(t % 2 + 1) * D], hT[:, f, t * T:(t + 1) * T],
                                       wd[:, f, :], start=(f == 0), stop=(f == FC - 1))
                mm.then_inc(d_full, 1)

        @block.tensor
        def _(pe):
            pe.wait_ge(consts_in, CONSTS)
            pe.wait_ge(picks_ready, 1)
            for t, _, n in TC:
                at = 128 * t if t < 8 else 1024
                mm = pe.transpose(psum[0:NP, at // 512, at % 512:at % 512 + 128],
                                  tie[:, t * B:(t + 1) * B, :].rearrange("p b e -> p (b e)"), ident[:])
            mm.then_inc(picks_turned, 1)
            pe.wait_ge(ranked, 1)
            pe.matmul(psum[0:NP, 3, 0:1], before[:], rank[:, SEQ - 1:SEQ], start=True, stop=True)
            pe.matmul(psum[0:NP, 3, 1:2], same[:], rank[:, SEQ - 1:SEQ], start=True, stop=True).then_inc(sums, 1)
            pe.wait_ge(chunks_ready, 1)
            pe.matmul(psum[0:NP, 4, 0:1], lower[:], small[:, 3:4], start=True, stop=True).then_inc(sums, 1)
            pe.wait_ge(reached_ready, 1)
            pe.matmul(psum[:, 5, 0:NCH], firsts[:], reached[:], start=True, stop=True).then_inc(sums, 1)
            pe.wait_ge(slots_ready, 1)
            for t, at, n in TC:
                mm = pe.transpose(psum[0:n, t // 8, (t % 8) * NP:(t % 8 + 1) * NP], rank[:, at:at + n],
                                  ident[0:NP, 0:NP])
            mm.then_inc(slots_turned, 1)
            pe.matmul(LISTS, zerob[:, 0:128], zerob[:], start=True, stop=False, skip_group_check=True)
            pe.wait_ge(lists_ready, 1)
            with pe.Fori(0, B) as b:
                shared_up(pe, b)
                pe.wait_ge(hot_ready, b + 1)
                for k in range(NK):
                    mm = pe.matmul(LISTS, hot_lo[:, k, :], hot_hi[:, k, :], start=False, stop=False,
                                   skip_group_check=True)
                mm.then_inc(hot_used, 1)
                shared_down(pe, b)
            pe.matmul(LISTS, zerob[:, 0:128], zerob[:], start=False, stop=True, skip_group_check=True) \
                .then_inc(lists_full, 1)

        @block.scalar
        def _(act):
            act.wait_ge(exp_in, 1)
            act.activation(expd[:], pick[:], ACT.Exp).then_inc(exp_ready, 1)
            with act.Fori(0, B) as b:
                for s, (at, w) in enumerate(CUTS):
                    for f in range(FC):
                        j = s * FC + f
                        act.wait_ge(g_full, b * UP + (j + 1))
                        act.wait_ge(hT_ready, b * UP + max(j - 1, 0))
                        act.activation(silu[:, j % 2, 0:w], psum[:, 2 * (j % 2), 0:w], ACT.Silu).then_inc(silu_ready, 1)

        @block.vector
        def _(dve):
            done = [0]

            def then(ins):
                ins.then_inc(step, 1)
                done[0] += 1

            def ordered():
                dve.wait_ge(step, done[0])

            wide = lambda a: a.unsqueeze(2).to_broadcast([128, N, E1])
            every = lambda a: a.unsqueeze(1).to_broadcast([128, N, E1])
            dve.wait_ge(consts_in, CONSTS)
            dve.wait_ge(zeroed, 4)
            dve.tensor_copy(iota_lo[:], iotas32[:, 0:128])
            dve.tensor_copy(iota_hi[:], iotas32[:, 128:])
            dve.tensor_copy(codes[:].rearrange("p a b k -> p a (b k)"), codes32[:]).then_inc(tables, 1)
            then(dve.tensor_reduce(best[:], logits, AX_X, ALU.max))
            ordered()
            dve.tensor_tensor(pick[:], logits, wide(best[:]), ALU.subtract).then_inc(exp_in, 1)
            dve.wait_ge(exp_ready, 1)
            then(dve.tensor_reduce(best[:], expd[:], AX_X, ALU.add))
            ordered()
            then(dve.reciprocal(best[:], best[:]))
            ordered()
            then(dve.tensor_tensor(score[:], expd[:], wide(best[:]), ALU.mult))
            ordered()
            then(dve.tensor_tensor(pick[:], score[:], every(ebias[:]), ALU.add))
            ordered()
            for n in range(2):
                then(dve.tensor_reduce(best[:], pick[:], AX_X, ALU.max))
                ordered()
                then(dve.tensor_tensor(tie[:], pick[:], wide(best[:]), ALU.is_equal))
                ordered()
                then(dve.tensor_tensor(tie[:], tie[:], every(order[:]), ALU.mult))
                ordered()
                then(dve.tensor_reduce(best[:], tie[:], AX_X, ALU.max))
                ordered()
                then(dve.tensor_tensor(picked[n][:], wide(best[:]), every(order[:]), ALU.is_equal))
                ordered()
                if n == 0:
                    then(dve.scalar_tensor_tensor(out=pick[:], in0=picked[0][:], scalar=-1e30, in1=pick[:],
                                                  op0=ALU.mult, op1=ALU.add))
                    ordered()
            dve.tensor_tensor(tie[:], picked[0][:], picked[1][:], ALU.add).then_inc(picks_ready, 1)
            dve.wait_ge(picks_ready, 1)
            then(dve.tensor_tensor(score[:], score[:], tie[:], ALU.mult))
            ordered()
            then(dve.tensor_reduce(best[:], score[:], AX_X, ALU.add))
            ordered()
            then(dve.tensor_scalar(best[:], best[:], 1e-9, None, ALU.add))
            ordered()
            then(dve.reciprocal(best[:], best[:]))
            ordered()
            dve.tensor_tensor(expd[:], score[:], wide(best[:]), ALU.mult).then_inc(shares_ready, 1)
            dve.wait_ge(picks_turned, 1)
            dve.tensor_copy(mask[:, 0:512], psum[0:NP, 0, :])
            dve.tensor_copy(mask[:, 512:CTX], psum[0:NP, 1, 0:CTX - 512])
            then(dve.tensor_copy(mask[:, CTX:SEQ], psum[0:NP, 2, 0:LAT]))
            ordered()
            dve.tensor_tensor_scan(rank[:], ones[:], mask[:], 0.0, ALU.mult, ALU.add).then_inc(ranked, 1)
            earlier, whole, lack, n_chunks, base, end = (small[:, k:k + 1] for k in range(6))
            dve.wait_ge(sums, 1)
            then(dve.tensor_copy(earlier, psum[0:NP, 3, 0:1]))
            then(dve.tensor_scalar(whole, psum[0:NP, 3, 1:2], 1.0 / WS, (WS - 1.0) / WS - 0.5 + 0.5 / WS,
                                   ALU.mult, ALU.add))
            ordered()
            dve.tensor_scalar(n_chunks, whole, ROUND, -ROUND, ALU.add, ALU.add).then_inc(chunks_ready, 1)
            dve.wait_ge(chunks_ready, 1)
            dve.wait_ge(sums, 2)
            then(dve.tensor_copy(base, psum[0:NP, 4, 0:1]))
            ordered()
            then(dve.tensor_tensor(end, base, n_chunks, ALU.add))
            then(dve.scalar_tensor_tensor(out=lack, in0=base, scalar=float(WS), in1=earlier, op0=ALU.mult, op1=ALU.add))
            ordered()
            dve.tensor_scalar(reached[:], chunks[:], end, None, ALU.is_ge).then_inc(reached_ready, 1)
            dve.tensor_scalar(rank[:], rank[:], lack, -1.0, ALU.add, ALU.add).then_inc(slots_ready, 1)
            dve.wait_ge(sums, 3)
            then(dve.tensor_scalar(expert[:], psum[:, 5, 0:NCH], float(E1 - 1), None, ALU.min))
            ordered()
            then(dve.tensor_copy(chunk_expert, expert[0:1, :]))
            then(dve.tensor_tensor(chunk_hot, expert[:].unsqueeze(2).to_broadcast([128, NCH, E1]),
                                   iotas32[:, 0:E1].unsqueeze(1).to_broadcast([128, NCH, E1]), ALU.is_equal))
            dve.wait_ge(slots_turned, 1)
            by_tile = slot[:].rearrange("p (t b) e -> p t (b e)", b=B)
            dve.tensor_copy(by_tile[:, 0:7, :], psum[:, 0, 0:7 * NP].rearrange("p (t n) -> p t n", n=NP))
            dve.tensor_copy(by_tile[0:CTX - 896, 7, :], psum[0:CTX - 896, 0, 7 * NP:8 * NP])
            then(dve.tensor_copy(by_tile[0:LAT, 8, :], psum[0:LAT, 1, 0:NP]))
            ordered()
            for n in range(2):
                then(dve.tensor_tensor(picked[n][:], picked[n][:], slot[:], ALU.mult))
            ordered()
            for n in range(2):
                then(dve.tensor_reduce(sel[:, :, n, :].rearrange("p b t -> p t b"),
                                       picked[n][:].rearrange("p (t b) e -> p t b e", b=B), AX_X, ALU.add))
            ordered()
            slots_of = sel[:].rearrange("p b n t -> p b (n t)")
            then(dve.tensor_scalar(hi32[:], slots_of, 1.0 / 128, 1.0 / 256 - 0.5, ALU.mult, ALU.add))
            ordered()
            then(dve.tensor_scalar(hi32[:], hi32[:], ROUND, -ROUND, ALU.add, ALU.add))
            ordered()
            dve.scalar_tensor_tensor(out=lo[:], in0=hi32[:], scalar=-128.0, in1=slots_of, op0=ALU.mult, op1=ALU.add)
            dve.tensor_copy(hi[:], hi32[:]).then_inc(lists_ready, 1)
            dve.wait_ge(lists_ready, 1)
            dve.wait_ge(tables, 1)
            with dve.Fori(0, B) as b:
                dve.wait_ge(hot_used, b)
                dve.wait_ge(hot_ready, b)
                here = lambda a: a[:, bass.ds(b, 1), :].rearrange("p b k -> p (b k)").unsqueeze(2)
                dve.tensor_tensor(hit[:], here(hi).to_broadcast([128, NK, NSL]),
                                  iota_hi[:].unsqueeze(1).to_broadcast([128, NK, NSL]), ALU.is_equal).then_inc(hit_ready, 1)
                dve.wait_ge(d_full, b * NB)
                for s, (at, w) in enumerate(CUTS):
                    for f in range(FC):
                        j = s * FC + f
                        dve.wait_ge(silu_ready, b * UP + (j + 1))
                        dve.wait_ge(u_full, b * UP + (j + 1))
                        dve.tensor_tensor(hT[:, f, at:at + w], silu[:, j % 2, 0:w], psum[:, 2 * (j % 2) + 1, 0:w],
                                          ALU.mult).then_inc(hT_ready, 1)
                    if s == 0:
                        dve.tensor_tensor(hot_lo[:], here(lo).to_broadcast([128, NK, 128]),
                                          iota_lo[:].unsqueeze(1).to_broadcast([128, NK, 128]), ALU.is_equal)
                        dve.wait_ge(hit_ready, b + 1)
                    elif s == 1:
                        dve.tensor_tensor(hot_hi[:, :, 0:NSL], hit[:], here(codes[:, 0]).to_broadcast([128, NK, NSL]),
                                          ALU.mult)
                dve.tensor_tensor(hot_hi[:, :, NSL:], hit[:], here(codes[:, 1]).to_broadcast([128, NK, NSL]),
                                  ALU.mult).then_inc(hot_ready, 1)
                dve.wait_ge(h_loaded, b * 16 + 16)
                dve.wait_ge(y_stored, b * 16)
                for p in range(NB):
                    dve.wait_ge(d_full, b * NB + (p + 1))
                    dve.tensor_tensor(y_out[:, 2 * p:2 * p + 2, :],
                                      psum[0:T, 4 + p % 2, 0:2 * D].rearrange("p (t d) -> p t d", t=2),
                                      h_in[:, 2 * p:2 * p + 2, :], ALU.add).then_inc(y_ready, 1)
            dve.wait_ge(lists_full, 1)
            dve.tensor_scalar(low_part[:], LISTS[:, NSL:], float(PAD - 128), None, ALU.add)
            then(dve.tensor_scalar(no_token[:], LISTS[:, 0:NSL], 0.0, None, ALU.is_equal))
            ordered()
            then(dve.scalar_tensor_tensor(out=rows[:], in0=LISTS[:, 0:NSL], scalar=128.0, in1=low_part[:],
                                          op0=ALU.mult, op1=ALU.add))
            then(dve.tensor_tensor(no_token[:], no_token[:], padrow[:], ALU.mult))
            ordered()
            then(dve.tensor_tensor(ids, rows[:], no_token[:], ALU.add))
            ordered()


def phase_mixture(nc, psum, inp, xg, y, ids, chunk_expert, chunk_hot):
    FC = F1 // 128
    ROWW = D + E1
    NP = GS // 2
    with ExitStack() as ctx:
        sb, sem = names(ctx, nc)
        ident = sb("mx_ident", [128, 128])
        wg = sb("mx_wg", [DP, 2, DC, F1])
        wu = sb("mx_wu", [DP, 2, DC, F1])
        wd = sb("mx_wd", [128, 2, FC, D])
        pad = sb("mx_pad", [128, 16])
        idx = sb("mx_idx", [128, 2, GS], I32)
        to = sb("mx_to", [128, 2, GS], I32)
        xs = sb("mx_xs", [128, 2, GS, ROWW])
        hot_share = sb("mx_hot_share", [128, GS, E1])
        share = sb("mx_share", [128, 2, GS])
        xT = sb("mx_xT", [DP, DC, WS])
        silu = sb("mx_silu", [128, 2, WS])
        hT = sb("mx_hT", [128, FC, WS])
        ys = sb("mx_ys", [128, 2, GS, D])
        ident_in = sem("mx_ident_in")
        weights_in = [sem("mx_weights_in0"), sem("mx_weights_in1")]
        idx_ready, to_ready = sem("mx_idx_ready"), sem("mx_to_ready")
        gathered = [sem("mx_gathered0"), sem("mx_gathered1")]
        product_ready, share_ready = sem("mx_product_ready"), sem("mx_share_ready")
        xT_full, xT_ready = sem("mx_xT_full"), sem("mx_xT_ready")
        g_full, u_full = sem("mx_g_full"), sem("mx_u_full")
        silu_ready, hT_ready = sem("mx_silu_ready"), sem("mx_hT_ready")
        d_full, ys_ready = sem("mx_d_full"), sem("mx_ys_ready")
        used = [sem("mx_used0"), sem("mx_used1")]
        added = sem("mx_added")
        GATHER = 16 * GS

        block = ctx.enter_context(nc.Block())

        @block.sync
        def _(sp):
            sp.dma_start(ident[:], inp["ident"]).then_inc(ident_in, 16)
            with sp.Fori(0, NCH // 2) as i:
                for half in range(2):
                    c = i * 2 + half
                    sp.wait_ge(used[half], i)
                    e = nc.values_load(chunk_expert[0:1, bass.ds(c, 1)], engines=[mybir.EngineType.SP],
                                       min_val=0, max_val=E1 - 1)
                    for dst, src, n in ((wg, "e1_gT", DC), (wu, "e1_uT", DC), (wd, "e1_dT", FC)):
                        sp.dma_start(dst[:, half], inp[src][bass.ds(e, 1)].rearrange("a (c p) n -> p (a c) n", c=n)) \
                            .then_inc(weights_in[half], 16)

        @block.gpsimd
        def _(pool):
            def carry(k):
                pool.tensor_tensor(pad[:, k:k + 1], ident[:, 0:1], ident[:, 0:1], ALU.add)

            pool.wait_ge(ident_in, 16)

            def gather(c, half, turned=True):
                if turned:
                    carry(14 + half)
                pool.tensor_copy(idx[:, half, :], ids[:, bass.ds(c * GS, GS)]).then_inc(idx_ready, 1)
                pool.wait_ge(idx_ready, c + 1)
                if turned:
                    pool.wait_ge(xT_full, (c - 1) * DC)
                    pool.wait_ge(share_ready, c - 1)
                carry(half * 6)
                for t in range(GS):
                    pool.indirect_dma_start(xs[:, half, t, :], None, xg,
                                            bass.IndirectOffsetOnAxis(ap=idx[:, half, t:t + 1], axis=0)) \
                        .then_inc(gathered[half], 16)

            def scatter(c, half):
                pool.wait_ge(added, c * GATHER)
                carry(12 + half)
                pool.tensor_copy(to[:, half, :], ids[:, bass.ds(c * GS, GS)]).then_inc(to_ready, 1)
                pool.wait_ge(to_ready, c + 1)
                for t in range(GS):
                    if t % 2 == 0:
                        pool.wait_ge(ys_ready, c * NP + (t // 2 + 1))
                        carry(half * 6 + 1 + t // 2)
                    pool.indirect_dma_start(y, bass.IndirectOffsetOnAxis(ap=to[:, half, t:t + 1], axis=0),
                                            ys[:, half, t, :], None, compute_op=ALU.add).then_inc(added, 16)

            gather(0, 0, False)
            with pool.Fori(0, NCH // 2 - 1) as i:
                for half in range(2):
                    c = i * 2 + half
                    pool.wait_ge(gathered[1 - half], i * GATHER + GATHER * half)
                    gather(c + 1, 1 - half)
                    scatter(c, half)
            pool.wait_ge(gathered[1], (NCH // 2 - 1) * GATHER)
            gather(NCH - 1, 1)
            scatter(NCH - 2, 0)
            scatter(NCH - 1, 1)
            pool.wait_ge(added, NCH * GATHER)

        @block.tensor
        def _(pe):
            def turn(c, half):
                pe.wait_ge(xT_ready, c * DC)
                for m in range(DC):
                    for t in range(GS):
                        mm = pe.transpose(psum[0:DP, 6 + m, t * 128:(t + 1) * 128],
                                          xs[:, half, t, m * DP:(m + 1) * DP], ident[:])
                    mm.then_inc(xT_full, 1)

            def up(c, half):
                pe.wait_ge(xT_ready, c * DC + DC)
                for f in range(FC):
                    pair = 2 * ((f + half) % 2)
                    pe.wait_ge(hT_ready, c * FC + (f - 1)) if f else pe.wait_ge(hT_ready, c * FC)
                    for w, k0, full in ((wg, 0, g_full), (wu, 1, u_full)):
                        for k in range(DC):
                            mm = pe.matmul(psum[:, pair + k0, :], w[:, half, k, f * 128:(f + 1) * 128],
                                           xT[:, k, :], start=(k == 0), stop=(k == 1))
                        mm.then_inc(full, 1)

            def down(c, half):
                pe.wait_ge(hT_ready, c * FC + FC)
                pe.wait_ge(ys_ready, c * NP)
                for p in range(NP):
                    for t in (2 * p, 2 * p + 1):
                        for f in range(FC):
                            mm = pe.matmul(psum[:, 4 + p, (t % 2) * D:(t % 2 + 1) * D],
                                           hT[:, f, t * 128:(t + 1) * 128], wd[:, half, f, :],
                                           start=(f == 0), stop=(f == FC - 1))
                    mm.then_inc(d_full if p < NP - 1 else used[half], 1)

            pe.wait_ge(ident_in, 16)
            pe.wait_ge(gathered[0], GATHER)
            turn(0, 0)
            with pe.Fori(0, NCH // 2 - 1) as i:
                for half in range(2):
                    c = i * 2 + half
                    pe.wait_ge(weights_in[half], i * 48 + 48)
                    up(c, half)
                    pe.wait_ge(gathered[1 - half], i * GATHER + GATHER * (1 + half))
                    turn(c + 1, 1 - half)
                    down(c, half)
            pe.wait_ge(weights_in[0], 48 * NCH // 2)
            up(NCH - 2, 0)
            pe.wait_ge(gathered[1], GATHER * NCH // 2)
            turn(NCH - 1, 1)
            down(NCH - 2, 0)
            pe.wait_ge(weights_in[1], 48 * NCH // 2)
            up(NCH - 1, 1)
            down(NCH - 1, 1)

        @block.scalar
        def _(act):
            with act.Fori(0, NCH // 2) as i:
                for half in range(2):
                    c = i * 2 + half
                    for f in range(FC):
                        s = (f + half) % 2
                        act.wait_ge(g_full, c * FC + (f + 1))
                        act.wait_ge(hT_ready, c * FC + (f - 1)) if f else act.wait_ge(hT_ready, c * FC)
                        act.activation(silu[:, s, :], psum[:, 2 * s, :], ACT.Silu).then_inc(silu_ready, 1)

        @block.vector
        def _(dve):
            def take_rows(c, half, n_gathered):
                dve.wait_ge(gathered[half], n_gathered)
                dve.wait_ge(share_ready, c)
                dve.tensor_tensor(hot_share[:], xs[:, half, :, D:],
                                  chunk_hot[:, bass.ds(c, 1), :].to_broadcast([128, GS, E1]), ALU.mult) \
                    .then_inc(product_ready, 1)
                dve.wait_ge(product_ready, c + 1)
                dve.tensor_reduce(share[:, half, :], hot_share[:], AX_X, ALU.add).then_inc(share_ready, 1)
                for m in range(DC):
                    dve.wait_ge(xT_full, c * DC + (m + 1))
                    dve.tensor_copy(xT[:, m, :], psum[0:DP, 6 + m, :]).then_inc(xT_ready, 1)

            def hidden(c, half, n_used):
                dve.wait_ge(used[1 - half], n_used)
                for f in range(FC):
                    s = (f + half) % 2
                    dve.wait_ge(silu_ready, c * FC + (f + 1))
                    dve.wait_ge(u_full, c * FC + (f + 1))
                    dve.tensor_tensor(hT[:, f, :], silu[:, s, :], psum[:, 2 * s + 1, :], ALU.mult).then_inc(hT_ready, 1)

            def results(c, half, n_used):
                dve.wait_ge(share_ready, c + 1)
                for p in range(NP):
                    if p < NP - 1:
                        dve.wait_ge(d_full, c * (NP - 1) + (p + 1))
                    else:
                        dve.wait_ge(used[half], n_used)
                    dve.tensor_tensor(ys[:, half, 2 * p:2 * p + 2, :],
                                      psum[:, 4 + p, 0:2 * D].rearrange("p (b d) -> p b d", b=2),
                                      share[:, half, 2 * p:2 * p + 2].unsqueeze(2).to_broadcast([128, 2, D]),
                                      ALU.mult).then_inc(ys_ready, 1)

            take_rows(0, 0, GATHER)
            with dve.Fori(0, NCH // 2 - 1) as i:
                for half in range(2):
                    c = i * 2 + half
                    hidden(c, half, i + half)
                    take_rows(c + 1, 1 - half, i * GATHER + GATHER * (1 + half))
                    results(c, half, i + 1)
            hidden(NCH - 2, 0, NCH // 2 - 1)
            take_rows(NCH - 1, 1, GATHER * NCH // 2)
            results(NCH - 2, 0, NCH // 2)
            hidden(NCH - 1, 1, NCH // 2)
            results(NCH - 1, 1, NCH // 2)


def build(nc, inp, out):
    h0 = nc.dram_tensor("h0_rows", (TOK, D), F32, kind="Internal").ap()
    h1 = nc.dram_tensor("h1_rows", (TOK, D), F32, kind="Internal").ap()
    y = nc.dram_tensor("y_rows", (TOK, D), F32, kind="Internal").ap()
    xg = nc.dram_tensor("x1_rows", (TOK, D + E0), F32, kind="Internal").ap()
    qk_parts = nc.dram_tensor("qk_parts", (B, 3, 4, DP, SEQ), BF16, kind="Internal").ap()
    v_rows = nc.dram_tensor("v_rows", (TOK, HEADS * HV), F32, kind="Internal").ap()
    o_parts = nc.dram_tensor("o_parts", (B, QUADS, 128, SEQ), F32, kind="Internal").ap()
    recips = nc.dram_tensor("recips", (B, HEADS, SEQ), F32, kind="Internal").ap()
    h3 = nc.dram_tensor("h3_rows", (TOK, D), F32, kind="Internal").ap()
    h4 = nc.dram_tensor("h4_rows", (PAD + TOK, D), F32, kind="Internal").ap()
    xg3 = nc.dram_tensor("x3_rows", (PAD + TOK, D + E1), F32, kind="Internal").ap()
    with ExitStack() as ctx:
        psum = ctx.enter_context(nc.psum_tensor("psum", [128, 8, 512], F32))
        phase_patches(nc, psum, inp, h0)
        with nc.sbuf_tensor("ids", [T, E0, NC], I32) as ids:
            with nc.sbuf_tensor("x1T", [DP, DC, B, SEQ], F32) as x1T:
                phase_retention(nc, psum, inp, h0, h1, xg, x1T[:])
                phase_route(nc, psum, inp, h1, xg, x1T[:], y, ids[:])
            phase_experts(nc, psum, inp, xg, y, ids[:])
        phase_heads(nc, psum, inp, y, qk_parts, v_rows)
        phase_attend(nc, psum, inp, qk_parts, v_rows, o_parts)
        with nc.sbuf_tensor("slot_rows", [128, NSL], I32) as ids, \
                nc.sbuf_tensor("chunk_expert", [1, NCH], I32) as chunk_expert, \
                nc.sbuf_tensor("chunk_hot", [128, NCH, E1], F32) as chunk_hot:
            with nc.sbuf_tensor("x3T", [DP, DC, B, SEQ], F32) as x3T, \
                    nc.sbuf_tensor("logits", [128, NTC * B, E1], F32) as logits:
                phase_project(nc, psum, inp, o_parts, recips, y, h3, x3T[:], logits[:], xg3)
                phase_dispatch(nc, psum, inp, h3, x3T[:], logits[:], h4, xg3, ids[:], chunk_expert[:], chunk_hot[:])
            phase_mixture(nc, psum, inp, xg3, h4, ids[:], chunk_expert[:], chunk_hot[:])
        phase_output(nc, h4, out)


def phase_output(nc, h4, out):
    with ExitStack() as ctx:
        _, sem = names(ctx, nc)
        out_stored = sem("out_stored")
        block = ctx.enter_context(nc.Block())

        @block.sync
        def _(sp):
            src, dst = h4[PAD:PAD + TOK].rearrange("(b n) d -> b (n d)", b=B), out.rearrange("b n d -> b (n d)")
            for b in range(B):
                sp.dma_start(dst[b:b + 1].rearrange("a (p n) -> (a p) n", p=80), src[b:b + 1].rearrange("a (p n) -> (a p) n", p=80)) \
                    .then_inc(out_stored, 16)
            sp.wait_ge(out_stored, 16 * B)


def prepare(inputs):
    a = {n: np.ascontiguousarray(v) for n, v in inputs.items()}
    x = a.pop("x")
    for side, n, k in PATCH:
        g = 224 // side
        a[f"x{side}"] = np.ascontiguousarray(
            x.reshape(B, g, side, g, side, 3).transpose(2, 4, 5, 0, 1, 3).reshape(k, B, n))
    a["ident"] = np.eye(128, dtype=np.float32)
    i = np.arange(T)
    mask = np.where(i[None, :] >= i[:, None], ALPHA ** (i[None, :] - i[:, None]).clip(0), 0.0) / np.sqrt(D)
    a["ret_dmask"] = np.tile(mask, (1, HB)).astype(np.float32)
    a["ret_qdec"] = np.tile(ALPHA ** (i + 1) / np.sqrt(D), (DP, HB)).astype(np.float32)
    a["ret_kdec"] = (ALPHA ** (T - 1.0 - i)).astype(np.float32)[:, None]
    p = np.arange(128)
    same = (p[:, None] % E0) == (p[None, :] % E0)
    a["rt_same"] = same.astype(np.float32)
    a["rt_before"] = (same & (p[:, None] // E0 < p[None, :] // E0)).astype(np.float32)
    a["rt_iota"] = np.tile(np.concatenate([np.arange(1, T + 1), np.arange(NC), p // E0 * NC]), (T, 1)).astype(np.float32)
    a["rt_row"] = np.arange(T, dtype=np.float32)[:, None]
    flip = lambda w: np.ascontiguousarray(np.swapaxes(w, -1, -2))
    a["gateT"] = flip(a.pop("L0_ffn_gate_weight"))
    for new, old in (("sh_gT", "L0_ffn_Ws_g"), ("sh_uT", "L0_ffn_Ws_u"), ("sh_dT", "L0_ffn_Ws_d"),
                     ("e0_gT", "L0_ffn_Wg"), ("e0_uT", "L0_ffn_Wu"), ("e0_dT", "L0_ffn_Wd"),
                     ("routerT", "L1_ffn_w_router"), ("e1_gT", "L1_ffn_Wg"), ("e1_uT", "L1_ffn_Wu"), ("e1_dT", "L1_ffn_Wd"),
                     ("s1_gT", "L1_ffn_sg"), ("s1_uT", "L1_ffn_su"), ("s1_dT", "L1_ffn_sd")):
        a[new] = flip(a.pop(old))
    inv = (np.float32(1.0) / np.float32(10000.0) ** (np.arange(0, DH, 2, dtype=np.float32) / np.float32(DH)))
    f = np.arange((KT + 1) * 128, dtype=np.float32)[:, None] * inv[None, :].astype(np.float32)
    c, s = np.cos(f), np.sin(f)
    both = lambda l, r: np.concatenate([np.tile(np.concatenate([l, r], 1), (1, HEADS)) * np.float32(DH ** -0.5),
                                        np.tile(np.concatenate([l, r], 1), (1, HEADS))], 1).astype(np.float32)
    a["rope_cos"], a["rope_sin"] = both(c, c), both(-s, s)
    a["mix_order"] = np.tile(np.arange(E1, 0, -1), (128, 1)).astype(np.float32)
    p = np.arange(B * E1)
    image_of, expert_of = p // E1, p % E1
    a["di_before"] = ((expert_of[:, None] == expert_of) & (image_of[:, None] < image_of)).astype(np.float32)
    a["di_same"] = (expert_of[:, None] == expert_of).astype(np.float32)
    a["di_lower"] = ((image_of[:, None] == 0) & (expert_of[:, None] < expert_of)).astype(np.float32)
    a["di_firsts"] = np.tile((image_of == 0).astype(np.float32)[:, None], (1, 128))
    a["di_chunks"] = np.tile(np.arange(NCH, dtype=np.float32), (B * E1, 1))
    a["di_iotas"] = np.tile(np.concatenate([np.arange(128), np.arange(NSL)]).astype(np.float32), (128, 1))
    start = np.array([[b * SEQ + at for _, at, _ in TC] for b in range(B)])
    start = np.tile(start[:, None, :], (1, 2, 1)).reshape(-1)
    lane = np.arange(128)
    a["di_codes"] = np.stack([np.tile(start // 128 + 1, (128, 1)), start % 128 + lane[:, None]], 1).astype(np.float32)
    a["di_padrow"] = (np.arange(NSL) % GS * 128 + lane[:, None] - (PAD - 128.0)).astype(np.float32)
    return a


def kernel(**inputs):
    import concourse.bacc as bacc
    from concourse.bass_utils import run_bass_kernel_spmd as run

    nc = bacc.Bacc("TRN2", target_bir_lowering=False, num_devices=1)
    arrays = prepare({n: np.asarray(v) for n, v in inputs.items()})
    inp = {n: nc.dram_tensor(f"in_{n}", a.shape, mybir.dt.from_np(a.dtype), kind="ExternalInput").ap()
           for n, a in arrays.items()}
    out = nc.dram_tensor("out_h", (B, SEQ, D), F32, kind="ExternalOutput").ap()
    build(nc, inp, out)
    r = run(nc, [{f"in_{n}": a for n, a in arrays.items()}], core_ids=[0])
    return r.results[0]["out_h"]
```
